# Optimizing a Trainium2 kernel written in Bass

```python
import numpy as np
import jax
import jax.numpy as jnp

def _softmax(x, axis=-1):
    return jax.nn.softmax(x, axis=axis)

def _gelu(x):
    return jax.nn.gelu(x, approximate=True)

def _silu(x):
    return jax.nn.silu(x)

def _sigmoid(x):
    return jax.nn.sigmoid(x)

def _layernorm(x, axis=-1, eps=1e-05):
    m = jnp.mean(x, axis=axis, keepdims=True)
    v = jnp.var(x, axis=axis, keepdims=True)
    return (x - m) / jnp.sqrt(v + eps)

def _scatter_add(tgt, idx, src, axis=0):
    return tgt.at[idx].add(src)

def _segment_sum(src, seg, n):
    return jax.ops.segment_sum(src, seg, n)
kernel_name = 'mk_gnn_resnorm_d1_gnn_r8_02b777'

def setup_inputs(seed: int=0):
    np.random.seed(seed)
    _w = jnp.asarray

    def _rec_inputs():
        import jax
        import jax.numpy as jnp
        _gk = jax.random.key(seed)
        x = -0.000202 + 1 * jax.random.normal(jax.random.fold_in(_gk, 1), (12500, 128), jnp.float32)
        src = jax.random.randint(jax.random.fold_in(_gk, 2), (400000,), 0, 12500, jnp.int32)
        dst = jnp.minimum((12500 * jax.random.uniform(jax.random.fold_in(_gk, 3), (400000,)) ** 2.0).astype(jnp.int32), 99999)
        _o = jnp.argsort(dst, stable=True)
        src = src[_o]
        dst = dst[_o]
        return (x, src, dst)
    x, src, dst = _rec_inputs()

    def _L0_gnn_setup():
        import jax, jax.numpy as jnp
        import numpy as np
        N_NODES = 6250
        N_EDGES = 100000
        D_MODEL = 128
        N_HEAD = 8
        key = jax.random.key(seed)
        k1, k2, k3, k4, k5 = jax.random.split(key, 5)
        scale = 1.0 / np.sqrt(D_MODEL)
        return {'embeds': jax.random.normal(k1, (N_NODES, D_MODEL), dtype=jnp.float32), 'edge_index': jax.random.randint(k2, (2, N_EDGES), 0, N_NODES, dtype=jnp.int64), 'qTrans': jax.random.normal(k3, (D_MODEL, D_MODEL), dtype=jnp.float32) * scale, 'kTrans': jax.random.normal(k4, (D_MODEL, D_MODEL), dtype=jnp.float32) * scale, 'vTrans': jax.random.normal(k5, (D_MODEL, D_MODEL), dtype=jnp.float32) * scale, 'ln_scale': jnp.ones((D_MODEL,), dtype=jnp.float32), 'ln_bias': jnp.zeros((D_MODEL,), dtype=jnp.float32)}
    _L0_gnn_all = _L0_gnn_setup()
    _L0_gnn_in = {k: v for k, v in _L0_gnn_all.items() if k in ('qTrans', 'kTrans', 'vTrans', 'ln_scale', 'ln_bias')}
    del _L0_gnn_all
    return {'x': x, 'src': src, 'dst': dst, 'L0_gnn_qTrans': _L0_gnn_in['qTrans'], 'L0_gnn_kTrans': _L0_gnn_in['kTrans'], 'L0_gnn_vTrans': _L0_gnn_in['vTrans'], 'L0_gnn_ln_scale': _L0_gnn_in['ln_scale'], 'L0_gnn_ln_bias': _L0_gnn_in['ln_bias']}

def reference(x, src, dst, L0_gnn_qTrans, L0_gnn_kTrans, L0_gnn_vTrans, L0_gnn_ln_scale, L0_gnn_ln_bias):
    import jax
    import jax.numpy as jnp

    def _L0_gnn_ref(embeds, edge_index, qTrans, kTrans, vTrans, ln_scale, ln_bias):
        import jax, jax.numpy as jnp
        import numpy as np
        N_NODES = 6250
        N_EDGES = 100000
        D_MODEL = 128
        N_HEAD = 8
        rows = edge_index[0]
        cols = edge_index[1]
        n, d = embeds.shape
        e = rows.shape[0]
        h = N_HEAD
        hd = d // h
        rowEmbeds = embeds[rows]
        colEmbeds = embeds[cols]
        q = (rowEmbeds @ qTrans).reshape(e, h, hd)
        k = (colEmbeds @ kTrans).reshape(e, h, hd)
        v = (colEmbeds @ vTrans).reshape(e, h, hd)
        att = jnp.einsum('ehd,ehd->eh', q, k)
        att = jnp.clip(att, -10.0, 10.0)
        expAtt = jnp.exp(att)
        attNorm = jax.ops.segment_sum(expAtt, rows, num_segments=n)[rows]
        att = expAtt / (attNorm + 1e-08)
        resEdges = (att[:, :, None] * v).reshape(e, d)
        res = jax.ops.segment_sum(resEdges, rows, num_segments=n)
        res = res + embeds
        mu = jnp.mean(res, axis=-1, keepdims=True)
        var = jnp.var(res, axis=-1, keepdims=True)
        out = (res - mu) * jax.lax.rsqrt(var + 1e-06) * ln_scale + ln_bias
        return out
    edge_index = jnp.stack([src, dst])
    x = _layernorm(x + _L0_gnn_ref(x, edge_index, L0_gnn_qTrans, L0_gnn_kTrans, L0_gnn_vTrans, L0_gnn_ln_scale, L0_gnn_ln_bias), axis=-1)
    return x

_drawn_inputs = setup_inputs


def setup_inputs(seed=0):
    import zlib

    import numpy as np

    out = dict(_drawn_inputs(seed))
    spreads = {'L0_gnn_ln_scale': (1.0, 0.2), 'L0_gnn_ln_bias': (0.0, 0.1)}
    factors = {}
    for name, (base, spread) in spreads.items():
        noise = np.random.default_rng([zlib.crc32(name.encode()), seed]).standard_normal(out[name].shape)
        drawn = base * np.exp(spread * noise) if base else spread * noise
        out[name] = jnp.asarray(drawn.astype(out[name].dtype))
    for name, factor in factors.items():
        out[name] = (out[name] * factor).astype(out[name].dtype)
    return out
```

```python
import concourse.bass as bass
from concourse import mybir
from contextlib import ExitStack

P = 128
NODES, EDGES, D, H = 12500, 400000, 128, 8
HD = D // H
NB = -(-NODES // P)
TAIL = NODES - (NB - 1) * P
ROW = 4096
LOG_ROW, LOG_P = 12, 7
FULL_ROWS = EDGES // ROW
REST = EDGES - FULL_ROWS * ROW
SENT_ROW = FULL_ROWS + 1
BPR = 4
SENT_COLS = BPR * P
PADB = BPR * (P - SENT_ROW)
assert PADB >= NB and P * ROW >= EDGES
LOC_SHIFT, BLK_SHIFT = 14, 22
KEY_BASE = 1 << 29
SENT_BIT = P << LOC_SHIFT
NO_BLOCK = P - 1
G = 4
TILES = -(-(-(-EDGES // P) + NB) // (4 * G)) * 4 * G
QUADS = TILES // G
ITERS = QUADS // 4
WD = D + H
KV = 2 * D
ORDER = [0, 4, 1, 5, 2, 6, 3, 7]
CH = 512
XC = 7
NCH = NB // XC
assert NCH * XC == NB


def flat(t, part_elems, off, dims):
    dims = [d for d in dims if d[1] > 1] or [[1, 1]]
    return bass.AP(t, off, [[part_elems, P]] + dims)


def bcast(v):
    return bass.AP(v.tensor, v.offset, [[0, P], [1, D]])


def build(nc, x, src, dst, wq, wk, wv, ln_scale, ln_bias, out):
    f32, bf16, i32 = mybir.dt.float32, mybir.dt.bfloat16, mybir.dt.int32
    ALU, ACT, AX = mybir.AluOpType, mybir.ActivationFunctionType, mybir.AxisListType
    ET = mybir.EngineType
    ctx = ExitStack()
    with ctx:
        def sb(name, shape, dt):
            return ctx.enter_context(nc.sbuf_tensor(name, shape, dt))

        def sem(name):
            return ctx.enter_context(nc.semaphore(name))

        kv_dram = nc.dram_tensor("kv_rows", [NB * P, KV], f32, kind="Internal").ap()

        q_parts = sb("q_parts", [P, NB * 3 * D], bf16)
        acc = sb("acc", [P, NB * WD], f32)
        keys = sb("keys", [P, 2 * ROW], f32)
        blk_row = sb("blk_row", [1, TILES], i32)
        kv = sb("kv", [P, 4, G, KV], f32)
        prod = sb("prod", [P, G * D], f32)
        wgt = sb("wgt", [P, 2, G, WD], f32)
        onehot = sb("onehot", [P, 4, G * P], bf16)
        onehot32 = sb("onehot32", [P, 2, G * P], f32)
        onehotT = sb("onehotT", [P, 2, G * P], bf16)
        att = sb("att", [P, 2, G * H], f32)
        ring = sb("ring", [P, 4, 2, G], i32)
        ident = sb("ident", [P, P], f32)
        ident16 = sb("ident16", [P, P], bf16)
        iota16 = sb("iota16", [P, P], bf16)
        ones = sb("ones", [P, P], f32)
        w_all = sb("w_all", [P, 3 * D], f32)
        xT = sb("xT", [P, 2, P], f32)
        x_tail = sb("x_tail", [P, D], f32)
        part_no = sb("part_no", [P, 1], i32)
        key_const = sb("key_const", [P, 1], i32)
        sign_i = sb("sign_i", [P, LOG_P], i32)
        sign = sb("sign", [P, LOG_P], f32)
        blk_base = sb("blk_base", [P, 1], f32)
        last_step = sb("last_step", [P, 1], f32)
        small_i = sb("small_i", [P, 2], i32)

        src_in = acc[:, 0:ROW].bitcast(i32)
        dst_in = acc[:, ROW:2 * ROW].bitcast(i32)
        E2 = EDGES // P
        src_cnt = acc[:, 2 * ROW:2 * ROW + E2].bitcast(i32)
        junk = acc[:, 2 * ROW + E2:2 * ROW + E2 + (E2 + 1) // 2].bitcast(bf16)
        assert 2 * ROW + E2 + (E2 + 1) // 2 <= NB * WD
        xs = kv[:, :, :, :].rearrange("p a b c -> p (a b c)")[:, 0:2 * XC * D].rearrange("p (s b d) -> p s b d", s=2, b=XC)
        qkv = wgt[:, :, :, :].rearrange("p a b c -> p (a b c)")[:, 0:2 * 3 * D].rearrange("p (s c) -> p s c", s=2)
        q_rest = onehot32[:, 0, 0:2 * D].rearrange("p (s c) -> p s c", s=2)
        cnt = onehot32[:, 1, 0:NB + 1]
        thr = onehot32[:, 1, P:P + NB + 1]
        mask = onehot[:, :, :].rearrange("p a b -> p (a b)").bitcast(f32)[:, 0:BPR * PADB].rearrange("p (i b) -> p i b", i=BPR)
        cnt_f = prod[:, 0:P]
        cnt_i = prod[:, P:2 * P].bitcast(i32)
        pad = onehot32[:, 1, 2 * P:2 * P + PADB]
        padsel = onehotT[:, :, :].rearrange("p a b -> p (a b)").bitcast(f32)[:, 0:BPR * PADB].rearrange("p (i b) -> p i b", i=BPR)
        cut = att[:, 0, 0:BPR]
        cut_raw = att[:, 0, BPR:2 * BPR]
        kv_flat = kv[:, :, :, :].rearrange("p a b c -> p (a b c)")
        s_col = kv_flat[:, 2048:2048 + SENT_COLS]
        s_val = kv_flat[:, 2560:2560 + SENT_COLS]

        psum = ctx.enter_context(nc.psum_tensor("psum", [P, 8 * CH], f32))

        def bank(n):
            return psum[:, n * CH:(n + 1) * CH]

        consts = sem("consts")
        const_v = sem("const_v")
        fill = sem("fill")
        src_in_s, dst_in_s, cnt_in_s = sem("src_loaded"), sem("dst_loaded"), sem("cnt_loaded")
        w_in, tail_in = sem("w_loaded"), sem("x_tail_loaded")
        x_in = [sem("x_loaded_0"), sem("x_loaded_1")]
        settled_p, settled_v = sem("settled_pool"), sem("settled_dve")
        chain_v = sem("dve_step")
        chain_p = sem("pool_step")
        counted, totals = sem("counted"), sem("totals")
        cuts_ready, sents_ready, sents_in = sem("cuts_ready"), sem("sents_ready"), sem("sents_in")
        sort11 = sem("rows_before_sentinels")
        xt_psum, xt_sb, proj, qkv_sb, q_split = (sem(n) for n in ("xt_psum", "xt_sb", "projected", "qkv_in_sbuf", "q_split"))
        kv_out = [sem("kv_stored_0"), sem("kv_stored_1")]
        c_sorted, c_flipped, c_moved = sem("chunk_sorted"), sem("chunk_flipped"), sem("chunk_moved")
        decoded = sem("decoded")
        acc_zero = sem("acc_zero")
        ring_ready, oh_ready, t_ready, ohT_ready, oh32_ready = (sem(n) for n in ("ring_ready", "onehot_ready", "transposed", "onehotT_ready", "onehot32_ready"))
        q_ready, seg_ready, exp_ready = sem("q_gathered"), sem("seg_summed"), sem("exp_ready")
        att_done, w_done, acc_done = sem("att_clipped"), sem("weighted"), sem("accumulated")
        gathered = [sem(f"kv_gathered_{n}") for n in range(4)]
        xf_in = [sem("x_again_0"), sem("x_again_1")]
        sc_in = sem("scale_loaded")
        stored = [sem("out_stored_0"), sem("out_stored_1")]
        var1, std1, coef1, norm1, res2, var2, std2, coef2, norm2 = (sem(n) for n in (
            "var1", "std1", "coef1", "norm1", "res2", "var2", "std2", "coef2", "norm2"))
        block = ctx.enter_context(nc.Block())

        def side(buf):
            return buf * ROW

        NTR = 2 * LOG_P + 1

        def plan():
            steps = [("rows", k, j) for k in range(1, LOG_ROW) for j in range(k - 1, -1, -1)]
            steps.append(("sentinels", 0, 0))
            steps += [("rows", LOG_ROW, j) for j in range(LOG_ROW - 1, -1, -1)]
            n = 0
            for k in range(LOG_ROW + 1, LOG_ROW + LOG_P + 1):
                steps.append(("flip", n, k))
                steps += [("cols", k, j) for j in range(k - 1, LOG_ROW - 1, -1)]
                steps.append(("flip", n + 1, k))
                steps += [("rows", k, j) for j in range(LOG_ROW - 1, -1, -1)]
                n += 2
            steps.append(("flip", n, 0))
            return steps

        PLAN = plan()

        def buffers():
            at, found = 0, []
            for kind, _, _ in PLAN:
                found.append(at)
                if kind != "sentinels":
                    at = 1 - at
            return found + [at]

        BUF = buffers()
        FLIPS = [(s, PLAN[s][1], PLAN[s][2]) for s in range(len(PLAN)) if PLAN[s][0] == "flip"]
        assert len(FLIPS) == NTR
        SENT_BUF = BUF[PLAN.index(("sentinels", 0, 0))]
        END = BUF[-1]
        IDX = 1 - END
        tiles_i = keys[:, side(END):side(END) + TILES].bitcast(i32)
        idx_i = keys[:, side(IDX):side(IDX) + TILES].bitcast(i32)

        def quad_columns(q):
            both = keys[:, :].bitcast(i32).rearrange("p (two c) -> p two c", two=2)
            return both[:, :, bass.ds(q * G, G)]

        FIRST_IS_IDX = IDX == 0
        R_IDX, R_LOC = (0, 1) if FIRST_IS_IDX else (1, 0)

        def seg(j, t):
            return bank(4 + 2 * (j % 2) + t // 2)[:, (t % 2) * WD:(t % 2 + 1) * WD]

        def res(u):
            return keys[:, u * ROW:u * ROW + XC * D].rearrange("p (b d) -> p b d", b=XC)

        def res_b(u):
            return keys[:, u * ROW + XC * D:u * ROW + 2 * XC * D].rearrange("p (b d) -> p b d", b=XC)

        def stat(u):
            return keys[:, u * ROW + 2 * XC * D:u * ROW + 2 * XC * D + XC * 24].rearrange("p (b s) -> p b s", b=XC)

        scale_bc = prod[:, 0:D]
        bias_bc = prod[:, D:2 * D]

        @block.sync
        def _(sp):
            sp.wait_ge(fill, 2)
            for t, flat_in, done in ((src, src_in, src_in_s), (dst, dst_in, dst_in_s)):
                a = (FULL_ROWS // 16) * 16
                sp.dma_start(flat_in[0:a, :], t[0:a * ROW].rearrange("(p c) -> p c", c=ROW)).then_inc(done, 16)
                sp.dma_start(flat_in[a:FULL_ROWS, :], t[a * ROW:FULL_ROWS * ROW].rearrange("(p c) -> p c", c=ROW)).then_inc(done, 16)
                sp.dma_start(flat_in[FULL_ROWS:FULL_ROWS + 1, 0:REST], t[FULL_ROWS * ROW:EDGES].rearrange("(p c) -> p c", p=1)).then_inc(done, 16)
                if t is src:
                    sp.dma_start(src_cnt, src.rearrange("(p c) -> p c", p=P)).then_inc(cnt_in_s, 16)
            for n, w in enumerate((wq, wk, wv)):
                sp.dma_start(w_all[:, n * D:(n + 1) * D], w).then_inc(w_in, 16)
            sp.wait_ge(consts, 1)
            sp.dma_start(x_tail[0:TAIL, :], x[(NB - 1) * P:NODES, :]).then_inc(tail_in, 16)

            def load_x(c, nblocks, into, slot, done):
                rows = x[bass.ds(c * XC * P, nblocks * P), :]
                sp.dma_start(into[:, slot, 0:nblocks, :], rows.rearrange("(b p) d -> p b d", p=P)).then_inc(done, 16)

            load_x(0, XC, xs, 0, x_in[0])
            load_x(1, XC, xs, 1, x_in[1])

            def prep(i, last, before_last):
                for u in range(2 * XC):
                    b = i * (2 * XC) + u
                    sp.wait_ge(qkv_sb, b + 1)
                    sp.dma_start(kv_dram[bass.ds(b * P, P), :], qkv[:, u % 2, D:3 * D]).then_inc(kv_out[u % 2], 16)
                    if u % XC == XC - 1 and not last:
                        c = 2 * i + (2 if u < XC else 3)
                        sp.wait_ge(xt_psum, b + 1)
                        n = XC - 1 if before_last and u >= XC else XC
                        load_x(c, n, xs, u // XC, x_in[u // XC])

            with sp.Fori(0, NCH // 2 - 2) as i:
                prep(i, False, False)
            sp.wait_ge(sents_ready, 1)
            sp.wait_ge(sort11, 1)
            sp.dma_start(keys[SENT_ROW:P, side(SENT_BUF):side(SENT_BUF) + SENT_COLS],
                         s_val[SENT_ROW:P, :]).then_inc(sents_in, 16)
            prep(NCH // 2 - 2, False, True)
            prep(NCH // 2 - 1, True, False)

            sp.wait_ge(w_done, QUADS)
            sp.dma_start(scale_bc, bcast(ln_scale)).then_inc(sc_in, 16)
            sp.dma_start(bias_bc, bcast(ln_bias)).then_inc(sc_in, 16)

            def final(i, first, last):
                for u in range(2):
                    c = 2 * i + u
                    if not first:
                        sp.wait_ge(norm2, c - 1)
                    rows = XC if not (last and u == 1) else XC - 1
                    load_x(c, rows, xs, u, xf_in[u])
                    if rows < XC:
                        sp.dma_start(xs[0:TAIL, u, XC - 1, :], x[(NB - 1) * P:NODES, :]).then_inc(xf_in[u], 16)

                for u in range(2):
                    c = 2 * i + u
                    sp.wait_ge(norm2, c + 1)
                    rows = XC if not (last and u == 1) else XC - 1
                    to = out[bass.ds(c * XC * P, rows * P), :]
                    sp.dma_start(to.rearrange("(b p) d -> p b d", p=P), res(u)[:, 0:rows, :]).then_inc(stored[u], 16)
                    if rows < XC:
                        sp.dma_start(out[(NB - 1) * P:NODES, :], res(u)[0:TAIL, XC - 1, :]).then_inc(stored[u], 16)

            final(0, True, False)
            with sp.Fori(1, NCH // 2 - 1) as i:
                final(i, False, False)
            final(NCH // 2 - 1, False, True)
            sp.wait_ge(stored[0], 16 * (NCH // 2))
            sp.wait_ge(stored[1], 16 * (NCH // 2) + 16)

        @block.gpsimd
        def _(pool):
            steps = [0]

            def link(ins):
                steps[0] += 1
                ins.then_inc(chain_p, 1)
                pool.wait_ge(chain_p, steps[0])

            pool.memset(src_in[96:P, :], NO_BLOCK * P).then_inc(fill, 1)
            pool.wait_ge(fill, 1)
            pool.memset(dst_in[96:P, :], SENT_BIT).then_inc(fill, 1)
            pool.wait_ge(fill, 2)
            pool.memset(x_tail[:, :], 0.0).then_inc(consts, 1)
            pool.wait_ge(consts, 1)
            link(pool.iota(part_no[:, :], [[0, 1]], base=0, channel_multiplier=1))
            pool.memset(pad, 0.0).then_inc(consts, 1)
            pool.wait_ge(consts, 2)
            link(pool.memset(ident[:, :], 0.0))
            link(pool.memset(ones[:, :], 1.0))
            link(pool.affine_select(out=ident[:, :], in_=ident[:, :], compare_op=ALU.not_equal, fill=1.0, base=0,
                                    pattern=[[-1, P]], channel_multiplier=1))
            link(pool.tensor_copy(ident16[:, :], ident[:, :]))
            link(pool.iota(cnt_i[:, 0:P], [[1, P]], base=0, channel_multiplier=0))
            link(pool.tensor_copy(iota16[:, :], cnt_i[:, 0:P]))
            link(pool.iota(cnt_i[:, 0:NB + 1], [[-P, NB + 1]], base=0, channel_multiplier=0))
            link(pool.tensor_copy(thr, cnt_i[:, 0:NB + 1]))
            link(pool.tensor_scalar(thr, thr, 0.5, None, ALU.add))
            link(pool.memset(cnt[:, 0:1], float(E2)))
            link(pool.memset(cnt[:, NB:NB + 1], float(-E2)))
            for i in range(BPR):
                link(pool.memset(mask[:, i, :], 1.0))
                link(pool.affine_select(out=mask[:, i, :], in_=mask[:, i, :], compare_op=ALU.is_equal, fill=0.0,
                                        base=BPR * SENT_ROW - i, pattern=[[1, PADB]], channel_multiplier=-BPR))
            link(pool.iota(small_i[:, 0:1], [[0, 1]], base=-BPR * SENT_ROW, channel_multiplier=BPR))
            link(pool.iota(small_i[:, 1:2], [[0, 1]], base=NO_BLOCK - (BPR - 1) + BPR * SENT_ROW, channel_multiplier=-BPR))
            link(pool.tensor_copy(blk_base[:, :], small_i[:, 0:1]))
            pool.tensor_copy(last_step[:, :], small_i[:, 1:2]).then_inc(consts, 1)
            pool.wait_ge(consts, 3)

            def settle():
                pool.sem_inc(settled_p, 1)

            def split(i, base):
                for u in range(2 * XC):
                    b = i * (2 * XC) + u
                    n = b * 5 + base
                    q = qkv[:, u % 2, 0:D]

                    def part(k):
                        return q_parts[:, bass.ds(b * (3 * D) + k * D, D)]

                    pool.wait_ge(qkv_sb, b + 1)
                    pool.tensor_copy(part(0), q).then_inc(chain_p, 1)
                    pool.wait_ge(chain_p, n + 1)
                    settle()
                    pool.tensor_tensor(q_rest[:, 0, :], q, part(0), ALU.subtract).then_inc(chain_p, 1)
                    pool.wait_ge(chain_p, n + 2)
                    pool.tensor_copy(part(1), q_rest[:, 0, :]).then_inc(chain_p, 1)
                    pool.wait_ge(chain_p, n + 3)
                    settle()
                    pool.tensor_tensor(q_rest[:, 1, :], q_rest[:, 0, :], part(1), ALU.subtract).then_inc(chain_p, 1)
                    pool.wait_ge(chain_p, n + 4)
                    pool.tensor_copy(part(2), q_rest[:, 1, :]).then_inc(chain_p, 1)
                    pool.wait_ge(chain_p, n + 5)
                    pool.nop().then_inc(q_split, 1)

            EARLY = 2
            base = steps[0]
            with pool.Fori(0, EARLY) as i:
                split(i, base)
            steps[0] += EARLY * 2 * XC * 5

            pool.wait_ge(cuts_ready, 1)
            lo = 96
            col, val = s_col[lo:P, :], s_val[lo:P, :]
            link(pool.iota(col.bitcast(i32), [[1, SENT_COLS]], base=0, channel_multiplier=0))
            link(pool.tensor_copy(val, col.bitcast(i32)))
            link(pool.tensor_copy(col, val))
            link(pool.tensor_scalar(val, col, cut[lo:P, 0:1], blk_base[lo:P, :], ALU.is_ge, ALU.add))
            link(pool.tensor_scalar(onehot32[lo:P, 0, :], col, cut[lo:P, 1:2], None, ALU.is_ge))
            link(pool.tensor_tensor(val, val, onehot32[lo:P, 0, :], ALU.add))
            link(pool.tensor_scalar(onehot32[lo:P, 0, :], col, cut[lo:P, 2:3], None, ALU.is_ge))
            link(pool.tensor_tensor(val, val, onehot32[lo:P, 0, :], ALU.add))
            link(pool.tensor_scalar(onehot32[lo:P, 0, :], col, cut[lo:P, 3:4], last_step[lo:P, :], ALU.is_ge, ALU.mult))
            link(pool.tensor_tensor(val, val, onehot32[lo:P, 0, :], ALU.add))
            link(pool.tensor_scalar(col.bitcast(i32), val, float(1 << BLK_SHIFT), float(KEY_BASE + SENT_BIT), ALU.mult, ALU.add))
            pool.tensor_scalar(val, col, sign[lo:P, 0:1], None, ALU.mult).then_inc(sents_ready, 1)
            pool.wait_ge(sents_ready, 1)

            base = steps[0] - EARLY * 2 * XC * 5
            with pool.Fori(EARLY, NCH // 2) as i:
                split(i, base)
            pool.memset(acc[:, :], 0.0).then_inc(acc_zero, 1)

            for s in range(2):
                pool.wait_ge(kv_out[s], 16 * (NB // 2))

            def gather(i, first):
                for j in range(4):
                    q = i * 4 + j
                    pool.wait_ge(ring_ready, q + 1)
                    if not first:
                        pool.wait_ge(w_done, q - 3)
                    settle()
                    for t in range(G):
                        pool.indirect_dma_start(kv[:, j, t, :], None, kv_dram,
                                                bass.IndirectOffsetOnAxis(ap=ring[:, j, R_IDX, t:t + 1], axis=0)
                                                ).then_inc(gathered[j], 16)

            gather(0, True)
            with pool.Fori(1, ITERS) as i:
                gather(i, False)

            pool.wait_ge(sc_in, 32)

            def bc(v, n=XC):
                return v.unsqueeze(1).to_broadcast([P, n, D])

            def final(i):
                for u in range(2):
                    c = 2 * i + u
                    n = c * 2
                    pool.wait_ge(norm1, c + 1)
                    pool.tensor_tensor(res_b(u), res_b(u), bc(scale_bc), ALU.mult).then_inc(chain_p, 1)
                    pool.wait_ge(chain_p, total_split + n + 1)
                    pool.tensor_tensor(res_b(u), res_b(u), bc(bias_bc), ALU.add).then_inc(chain_p, 1)
                    pool.wait_ge(chain_p, total_split + n + 2)
                    pool.tensor_tensor(res_b(u), res_b(u), xs[:, u, :, :], ALU.add).then_inc(res2, 1)

            total_split = base + 5 * NB
            with pool.Fori(0, NCH // 2) as i:
                final(i)

        @block.scalar
        def _(act):
            act.wait_ge(chain_p, POOL_CONSTS)
            act.wait_ge(cnt_in_s, 16)
            with act.Fori(1, NB) as t:
                act.activation(junk[:, 0:E2], src_cnt, ACT.Sign, bias=thr[:, bass.ds(t, 1)], scale=1.0,
                               accum_out=cnt[:, bass.ds(t, 1)]).then_inc(counted, 1)
                act.wait_ge(counted, t)

            def prep(i, first):
                for u in range(2 * XC):
                    b = i * (2 * XC) + u
                    act.wait_ge(xt_psum, b + 1)
                    if not (first and u < 2):
                        act.wait_ge(proj, b - 1)
                    act.activation(xT[:, u % 2, :], bank(u % 2)[:, 0:P], ACT.Copy).then_inc(xt_sb, 1)
                    act.wait_ge(proj, b + 1)
                    if not (first and u < 2):
                        act.wait_ge(q_split, b - 1)
                        act.wait_ge(kv_out[u % 2], kv_count(i, u))
                    act.activation(qkv[:, u % 2, :], bank(2 + u % 2)[:, 0:3 * D], ACT.Copy).then_inc(qkv_sb, 1)

            def kv_count(i, u):
                return i * (16 * XC) + 16 * (u // 2)

            prep(0, True)
            with act.Fori(1, NCH // 2) as i:
                prep(i, False)

            for s, n, k in FLIPS:
                to = side(BUF[s + 1])
                into_rows = n % 2 == 1
                if n == NTR - 1:
                    act.wait_ge(c_flipped, 8 * NTR)
                for pos, c in enumerate(ORDER):
                    act.wait_ge(c_flipped, 8 * n + pos + 1)
                    if n == NTR - 1:
                        gs = CH // P
                        view = keys[:, to:to + ROW].rearrange("p (a g) -> p g a", g=ROW // P)[:, c * gs:(c + 1) * gs, :]
                        act.activation(view, bank(pos).rearrange("p (g a) -> p g a", g=gs), ACT.Copy).then_inc(c_moved, 1)
                    else:
                        signed = into_rows and k < LOG_ROW + LOG_P
                        sc = sign[:, k - LOG_ROW:k - LOG_ROW + 1] if signed else 1.0
                        act.activation(keys[:, to + c * CH:to + (c + 1) * CH], bank(pos), ACT.Copy, scale=sc).then_inc(c_moved, 1)

            act.wait_ge(decoded, 1)

            def copy_ring(q, j, gathers):
                if gathers is not None:
                    act.wait_ge(gathered[j], gathers)
                    act.wait_ge(oh_ready, q - 3)
                act.activation(ring[:, j, :, :], quad_columns(q), ACT.Copy).then_inc(ring_ready, 1)

            def expand(q, j, first2):
                act.wait_ge(oh_ready, q + 1)
                if not first2:
                    act.wait_ge(seg_ready, q - 1)
                act.activation(onehot32[:, j % 2, :], onehot[:, j % 4, :], ACT.Copy).then_inc(oh32_ready, 1)

            def exps(q, j, first2):
                act.wait_ge(att_done, q + 1)
                a = att[:, j % 2, :].rearrange("p (g h) -> p g h", g=G)
                act.activation(wgt[:, j % 2, :, D:WD], a, ACT.Exp).then_inc(exp_ready, 1)

            def move_T(q, j, first2):
                act.wait_ge(t_ready, q + 1)
                if not first2:
                    act.wait_ge(q_ready, q - 1)
                act.activation(onehotT[:, j % 2, :], bank(j % 2)[:, 0:CH // 2].bitcast(bf16), ACT.Copy).then_inc(ohT_ready, 1)

            for q in range(4):
                copy_ring(q, q, None)
            for q in range(3):
                move_T(q, q, q < 2)
                if q == 0:
                    expand(0, 0, True)
            exps(0, 0, True)

            def steps(i, first, last):
                for j in range(4):
                    s = i * 4 + j
                    if not last:
                        copy_ring(s + 4, j, i * (16 * G) + 16 * G)
                    if not (last and j == 3):
                        expand(s + 1, j + 1, first and j == 0)
                        exps(s + 1, j + 1, first and j == 0)
                    if not (last and j >= 1):
                        move_T(s + 3, j + 3, False)

            steps(0, True, False)
            with act.Fori(1, ITERS - 1) as i:
                steps(i, False, False)
            steps(ITERS - 1, False, True)

            def final(i):
                for u in range(2):
                    c = 2 * i + u
                    for n, (var, std, coef, norm, a, b) in enumerate(((var1, std1, coef1, norm1, res(u), res_b(u)),
                                                                     (var2, std2, coef2, norm2, res_b(u), res(u)))):
                        o = 12 * n
                        act.wait_ge(var, c + 1)
                        act.activation(stat(u)[:, :, o + 8], stat(u)[:, :, o + 7], ACT.Sqrt).then_inc(std, 1)
                        act.wait_ge(coef, c + 1)
                        if n == 1:
                            pass
                        for k in range(XC):
                            ins = act.activation(b[:, k, :], a[:, k, :], ACT.Identity, scale=stat(u)[:, k, o + 9:o + 10],
                                                 bias=stat(u)[:, k, o + 10:o + 11])
                        ins.then_inc(norm, 1)

            with act.Fori(0, NCH // 2) as i:
                final(i)

        @block.tensor
        def _(pe):
            pe.wait_ge(consts, 3)
            pe.wait_ge(counted, NB - 1)
            pe.matmul(bank(4)[:, 0:NB + 1], ones[:, :], cnt, start=True, stop=True).then_inc(totals, 1)
            pe.wait_ge(w_in, 48)
            pe.wait_ge(tail_in, 16)

            def turn(i, u, first, last):
                b = i * (2 * XC) + u
                if u % XC == 0:
                    pe.wait_ge(x_in[(u // XC) % 2], (i + u // (2 * XC)) * 16 + 16)
                if not (first and u < 2):
                    pe.wait_ge(xt_sb, b - 1)
                x_b = x_tail[:, :] if last and u == 2 * XC - 1 else xs[:, (u // XC) % 2, u % XC, :]
                pe.transpose(bank(u % 2)[:, 0:P], x_b, ident[:, :]).then_inc(xt_psum, 1)

            def project(i, first, last):
                for u in range(2 * XC):
                    b = i * (2 * XC) + u
                    if not (last and u == 2 * XC - 1):
                        turn(i, u + 1, first, last)
                    pe.wait_ge(xt_sb, b + 1)
                    if not (first and u < 2):
                        pe.wait_ge(qkv_sb, b - 1)
                    pe.matmul(bank(2 + u % 2)[:, 0:3 * D], xT[:, u % 2, :], w_all[:, :], start=True, stop=True).then_inc(proj, 1)

            turn(0, 0, True, False)
            project(0, True, False)
            with pe.Fori(1, NCH // 2 - 1) as i:
                project(i, False, False)
            project(NCH // 2 - 1, False, True)

            pe.wait_ge(qkv_sb, NB)
            for s, n, k in FLIPS:
                at = side(BUF[s])
                for pos, c in enumerate(ORDER):
                    pe.wait_ge(c_sorted, 8 * n + pos + 1)
                    if n:
                        pe.wait_ge(c_moved, 8 * (n - 1) + pos + 1)
                    for g in range(CH // P):
                        o = c * CH + g * P
                        ins = pe.transpose(bank(pos)[:, g * P:(g + 1) * P], keys[:, at + o:at + o + P], ident[:, :])
                    ins.then_inc(c_flipped, 1)
            pe.wait_ge(c_moved, 8 * NTR)
            pe.wait_ge(q_split, NB)
            pe.wait_ge(decoded, 1)

            def transposes(q, j, first2):
                pe.wait_ge(oh_ready, q + 1)
                if not first2:
                    pe.wait_ge(ohT_ready, q - 1)
                for t in range(G):
                    ins = pe.transpose(bank(j % 2)[:, t * P // 2:(t + 1) * P // 2].bitcast(bf16),
                                       onehot[:, j % 4, t * P:(t + 1) * P], ident16[:, :])
                ins.then_inc(t_ready, 1)

            def gather_q(q, j, blks, first2):
                pe.wait_ge(ohT_ready, q + 1)
                if not first2:
                    pe.wait_ge(att_done, q - 1)
                for t in range(G):
                    for k in range(3):
                        ins = pe.matmul(bank(2 + j % 2)[:, t * D:(t + 1) * D], onehotT[:, j % 2, t * P:(t + 1) * P],
                                        q_parts[:, bass.ds(blks[t] * (3 * D) + k * D, D)], start=(k == 0), stop=(k == 2))
                ins.then_inc(q_ready, 1)

            def segment_sum(q, j, first2):
                pe.wait_ge(w_done, q + 1)
                pe.wait_ge(oh32_ready, q + 1)
                if not first2:
                    pe.wait_ge(acc_done, (q - 1) * G)
                for t in range(G):
                    ins = pe.matmul(seg(j, t), onehot32[:, j % 2, t * P:(t + 1) * P], wgt[:, j % 2, t, :], start=True, stop=True)
                ins.then_inc(seg_ready, 1)

            def blocks(first_tile, n):
                return nc.values_load_multi_w_load_instructions(blk_row[0:1, bass.ds(first_tile, n)], engines=(ET.PE,),
                                                                min_val=0, max_val=NB - 1)[1]

            early = blocks(0, 2 * G)
            for q in range(3):
                transposes(q, q, q < 2)
                if q < 2:
                    gather_q(q, q, early[q * G:(q + 1) * G], True)

            def steps(i, first, last):
                blks = blocks(i * 16 + 2 * G, 2 * G if last else 4 * G)
                for j in range(4):
                    s = i * 4 + j
                    if not (last and j >= 2):
                        gather_q(s + 2, j + 2, blks[j * G:(j + 1) * G], False)
                    if not (last and j >= 1):
                        transposes(s + 3, j + 3, False)
                    segment_sum(s, j, first and j < 2)

            steps(0, True, False)
            with pe.Fori(1, ITERS - 1) as i:
                steps(i, False, False)
            steps(ITERS - 1, False, True)

        @block.vector
        def _(dve):
            steps_v = [0]

            def link(ins):
                steps_v[0] += 1
                ins.then_inc(chain_v, 1)
                dve.wait_ge(chain_v, steps_v[0])

            dve.wait_ge(chain_p, 1)
            for m in range(LOG_P):
                link(dve.tensor_scalar(sign_i[:, m:m + 1], part_no[:, :], m, 1, ALU.logical_shift_right, ALU.bitwise_and))
            link(dve.tensor_scalar(sign[:, :], sign_i[:, :], -2.0, 1.0, ALU.mult, ALU.add))
            link(dve.tensor_scalar(key_const[:, :], part_no[:, :], 31, KEY_BASE, ALU.logical_shift_left, ALU.bitwise_or))

            first = keys[:, side(BUF[0]):side(BUF[0]) + ROW].bitcast(i32)
            other = keys[:, side(1 - BUF[0]):side(1 - BUF[0]) + ROW].bitcast(i32)
            dve.wait_ge(src_in_s, 48)
            link(dve.tensor_scalar(first, src_in, (P - 1) << LOG_P, BLK_SHIFT - LOG_P, ALU.bitwise_and, ALU.logical_shift_left))
            link(dve.tensor_scalar(other, src_in, P - 1, LOC_SHIFT, ALU.bitwise_and, ALU.logical_shift_left))
            link(dve.tensor_tensor(first, first, other, ALU.bitwise_or))
            dve.wait_ge(dst_in_s, 48)
            link(dve.tensor_tensor(other, first, dst_in, ALU.bitwise_or))
            link(dve.tensor_scalar(first, other, key_const[:, 0:1], None, ALU.bitwise_or))

            def exchange(to, at, k, j, negated=False, c=None, width=CH):
                o = 0 if c is None else c * width
                n = ROW if c is None else width
                if k is None:
                    dims = mins = maxs = [[2 << j, n >> (j + 1)], [1, 1 << j]]
                else:
                    rest = [[2 << j, 1 << (k - 1 - j)], [1, 1 << j]]
                    hi = [2 << k, n >> (k + 1)]
                    dims = [hi, [1 << k, 2]] + rest
                    mins = [hi, [(1 << k) + (1 << j), 2]] + rest
                    maxs = [hi, [(1 << k) - (1 << j), 2]] + rest
                if k is not None and n >> (k + 1) > 1 and k - 1 - j > 0 and j > 0:
                    for r, first_op, second_op in ((0, ALU.min, ALU.max), (1 << k, ALU.max, ALU.min)):
                        own = [hi] + rest
                        a, b = (flat(keys, 2 * ROW, at + o + r + h, own) for h in (0, 1 << j))
                        dve.tensor_tensor(flat(keys, 2 * ROW, to + o + r, own), a, b, first_op)
                        ins = dve.tensor_tensor(flat(keys, 2 * ROW, to + o + r + (1 << j), own), a, b, second_op)
                    return ins
                a = flat(keys, 2 * ROW, at + o, dims)
                b = flat(keys, 2 * ROW, at + o + (1 << j), dims)
                low = flat(keys, 2 * ROW, to + o, mins)
                high = flat(keys, 2 * ROW, to + o + (1 << j), maxs)
                if negated:
                    runs = [(0, ALU.min, ALU.max)] if k is None else [(0, ALU.min, ALU.max), (1 << k, ALU.max, ALU.min)]
                    for r, first_op, second_op in runs:
                        ab = [[2 << j, n >> (j + 1)] if k is None else [2 << k, n >> (k + 1)], [1, 1 << j]]
                        lo_at, lo_to = at + o + r, to + o + r
                        a, b = (flat(keys, 2 * ROW, lo_at + h, ab) for h in (0, 1 << j))
                        dve.scalar_tensor_tensor(flat(keys, 2 * ROW, lo_to, ab), b, -1.0, a, ALU.mult, first_op)
                        ins = dve.scalar_tensor_tensor(flat(keys, 2 * ROW, lo_to + (1 << j), ab), b, -1.0, a, ALU.mult, second_op)
                    return ins
                dve.tensor_tensor(low, a, b, ALU.min)
                return dve.tensor_tensor(high, a, b, ALU.max)

            def exchange_halves(to, at, c):
                a, b = (keys[:, at + h + c * CH:at + h + (c + 1) * CH] for h in (0, ROW // 2))
                dve.tensor_tensor(keys[:, to + c * CH:to + (c + 1) * CH], a, b, ALU.min)
                return dve.tensor_tensor(keys[:, to + ROW // 2 + c * CH:to + ROW // 2 + (c + 1) * CH], a, b, ALU.max)

            def cut_rows():
                dve.wait_ge(totals, 1)
                dve.wait_ge(consts, 3)
                tot = padsel.rearrange("p i b -> p (i b)")[:, 0:NB + 1]
                link(dve.tensor_copy(tot, bank(4)[:, 0:NB + 1]))
                link(dve.tensor_tensor(cnt_f[:, 0:NB], tot[:, 0:NB], tot[:, 1:NB + 1], ALU.subtract))
                link(dve.tensor_scalar(cnt_i[:, 0:NB], cnt_f[:, 0:NB], 0.5, None, ALU.mult))
                link(dve.tensor_scalar(cnt_i[:, 0:NB], cnt_i[:, 0:NB], P - 1, None, ALU.bitwise_and))
                link(dve.tensor_scalar(cnt_i[:, 0:NB], cnt_i[:, 0:NB], -1.0, float(P), ALU.mult, ALU.add))
                link(dve.tensor_scalar(cnt_i[:, 0:NB], cnt_i[:, 0:NB], P - 1, None, ALU.bitwise_and))
                link(dve.tensor_copy(pad[:, 0:NB], cnt_i[:, 0:NB]))
                link(dve.tensor_tensor(padsel, mask, pad.unsqueeze(1).to_broadcast([P, BPR, PADB]), ALU.mult))
                link(dve.tensor_reduce(cut_raw, padsel, AX.X, ALU.add))
                link(dve.tensor_copy(cut[:, 0:1], cut_raw[:, 0:1]))
                for i in range(1, BPR):
                    ins = dve.tensor_tensor(cut[:, i:i + 1], cut[:, i - 1:i], cut_raw[:, i:i + 1], ALU.add)
                    if i < BPR - 1:
                        link(ins)
                ins.then_inc(cuts_ready, 1)

            for s, (kind, k, j) in enumerate(PLAN):
                at, to = side(BUF[s]), side(BUF[s + 1])
                if kind == "sentinels":
                    dve.nop().then_inc(sort11, 1)
                    dve.wait_ge(sents_in, 16)
                    continue
                if kind == "flip":
                    continue
                direction = k if kind == "rows" and k < LOG_ROW else None
                jj = j
                if kind == "cols":
                    direction, jj = (k - LOG_ROW if k < LOG_ROW + LOG_P else None), j - LOG_ROW
                before, after = PLAN[s - 1] if s else ("", 0, 0), PLAN[s + 1]
                chunked_in, chunked_out = before[0] == "flip", after[0] == "flip"
                if kind == "rows" and chunked_in:
                    for m in range(4):
                        dve.wait_ge(c_moved, 8 * before[1] + 2 * m + 2)
                        ins = exchange_halves(to, at, m)
                    link(ins)
                elif chunked_in or chunked_out:
                    for pos, c in enumerate(ORDER):
                        if chunked_in:
                            dve.wait_ge(c_moved, 8 * before[1] + pos + 1)
                        ins = exchange(to, at, direction, jj, negated=chunked_in, c=c)
                        if chunked_out:
                            ins.then_inc(c_sorted, 1)
                    if not chunked_out:
                        link(ins)
                else:
                    link(exchange(to, at, direction, jj))
                if (k, j) == (LOG_ROW - 2, 0):
                    cut_rows()

            dve.wait_ge(c_moved, 8 * NTR)
            link(dve.tensor_scalar(blk_row[:, :], tiles_i[0:1, :], BLK_SHIFT, P - 1, ALU.logical_shift_right, ALU.bitwise_and))
            link(dve.tensor_scalar(blk_row[:, :], blk_row[:, :], float(NB - 1), None, ALU.min))
            link(dve.tensor_scalar(idx_i, tiles_i, (1 << LOC_SHIFT) - 1, None, ALU.bitwise_and))
            dve.tensor_scalar(tiles_i, tiles_i, LOC_SHIFT, 2 * P - 1, ALU.logical_shift_right, ALU.bitwise_and).then_inc(decoded, 1)
            dve.wait_ge(decoded, 1)
            dve.wait_ge(acc_zero, 1)
            base_v = steps_v[0]

            def onehots(q, j, first):
                dve.wait_ge(ring_ready, q + 1)
                if not first:
                    dve.wait_ge(t_ready, q - 3)
                    dve.wait_ge(oh32_ready, q - 3)
                for t in range(G):
                    ins = dve.tensor_scalar(onehot[:, j % 4, t * P:(t + 1) * P], iota16[:, :],
                                            ring[:, j % 4, R_LOC, t:t + 1], None, ALU.is_equal)
                ins.then_inc(oh_ready, 1)

            def products(q, j, arrived):
                dve.wait_ge(gathered[j % 4], arrived)
                dve.wait_ge(q_ready, q + 1)
                p = prod[:, :].rearrange("p (g d) -> p g d", g=G)
                ps = bank(2 + j % 2).rearrange("p (g d) -> p g d", g=G)
                dve.tensor_tensor(p, kv[:, j % 4, :, 0:D], ps, ALU.mult).then_inc(chain_v, 1)

            def reduce_heads(q, j):
                dve.wait_ge(chain_v, base_v + 2 * q + 1)
                dve.tensor_reduce(att[:, j % 2, :], prod[:, :].rearrange("p (gh e) -> p gh e", e=HD), AX.X, ALU.add
                                  ).then_inc(chain_v, 1)

            def clip(q, j):
                dve.wait_ge(chain_v, base_v + 2 * q + 2)
                dve.tensor_scalar(att[:, j % 2, :], att[:, j % 2, :], -10.0, 10.0, ALU.max, ALU.min).then_inc(att_done, 1)

            def weight(q, j, first2):
                dve.wait_ge(exp_ready, q + 1)
                w = wgt[:, j % 2, :, 0:D].rearrange("p g (h e) -> p g h e", h=H)
                v = kv[:, j % 4, :, D:KV].rearrange("p g (h e) -> p g h e", h=H)
                e = wgt[:, j % 2, :, D:WD].unsqueeze(3).to_broadcast([P, G, H, HD])
                dve.tensor_tensor(w, v, e, ALU.mult).then_inc(w_done, 1)

            def accumulate(q, j, t, blks, first):
                if t == 0:
                    dve.wait_ge(seg_ready, q + 1)
                if not (first and t == 0):
                    dve.wait_ge(acc_done, q * G + t)
                a = acc[:, bass.ds(blks[t] * WD, WD)]
                dve.tensor_tensor(a, a, seg(j, t), ALU.add).then_inc(acc_done, 1)

            def blocks(first_tile, n):
                return nc.values_load_multi_w_load_instructions(blk_row[0:1, bass.ds(first_tile, n)], engines=(ET.DVE,),
                                                                min_val=0, max_val=NB - 1)[1]

            for q in range(3):
                onehots(q, q, True)
            products(0, 0, 64)
            reduce_heads(0, 0)
            clip(0, 0)

            def steps(i, first, last):
                blks = blocks(0, 2 * G) if first else blocks(i * 16 - 2 * G, 4 * G)
                for j in range(4):
                    s = i * 4 + j
                    old = not (first and j < 2)
                    b = (blks[(j - 2) * G:] if first else blks[j * G:])
                    new = not (last and j == 3)

                    def add(t):
                        if old:
                            accumulate(s - 2, j + 2, t, b, first and j == 2)

                    add(0)
                    if new:
                        products(s + 1, j + 1, (i + (j + 1) // 4) * 64 + 64)
                    add(1)
                    if new:
                        reduce_heads(s + 1, j + 1)
                    add(2)
                    if new:
                        clip(s + 1, j + 1)
                    add(3)
                    weight(s, j, first and j < 2)
                    if not (last and j >= 1):
                        onehots(s + 3, j + 3, first and j == 0)

            steps(0, True, False)
            with dve.Fori(1, ITERS - 1) as i:
                steps(i, False, False)
            steps(ITERS - 1, False, True)
            blks = blocks(TILES - 2 * G, 2 * G)
            for n in range(2):
                for t in range(G):
                    accumulate(QUADS - 2 + n, n, t, blks[n * G:], False)
            dve.wait_ge(acc_done, QUADS * G)

            total_v = base_v + 2 * QUADS

            def final(i, first, last):
                for u in range(2):
                    c = 2 * i + u
                    n = [0]

                    def step(ins):
                        n[0] += 1
                        ins.then_inc(chain_v, 1)
                        dve.wait_ge(chain_v, c * PER_CHUNK + (total_v + n[0]))

                    def count():
                        n[0] += 1
                        return n[0]

                    def reached(m):
                        dve.wait_ge(chain_v, c * PER_CHUNK + (total_v + m))

                    sums = acc[:, bass.ds(c * (XC * WD), XC * WD)].rearrange("p (b w) -> p b w", b=XC)
                    recip = stat(u)[:, :, 0:H]
                    if not first:
                        dve.wait_ge(stored[u], 16 * i)
                    step(dve.tensor_scalar(recip, sums[:, :, D:WD], 1e-8, None, ALU.add))
                    step(dve.reciprocal(recip, recip))
                    r4 = res(u).rearrange("p b (h e) -> p b h e", h=H)
                    s4 = sums[:, :, 0:D].rearrange("p b (h e) -> p b h e", h=H)
                    step(dve.tensor_tensor(r4, s4, recip.unsqueeze(3).to_broadcast([P, XC, H, HD]), ALU.mult))
                    dve.wait_ge(xf_in[u], 16 * (i + 1) + (16 if last and u == 1 else 0))
                    step(dve.tensor_tensor(res(u), res(u), xs[:, u, :, :], ALU.add))
                    stats(res(u), u, 0, 1e-6, step, count, reached)
                    dve.nop().then_inc(var1, 1)
                    dve.wait_ge(std1, c + 1)
                    coefs(u, 0, step)
                    dve.nop().then_inc(coef1, 1)
                    dve.wait_ge(res2, c + 1)
                    stats(res_b(u), u, 12, 1e-5, step, count, reached)
                    dve.nop().then_inc(var2, 1)
                    dve.wait_ge(std2, c + 1)
                    coefs(u, 12, step)
                    dve.nop().then_inc(coef2, 1)
                    assert n[0] == PER_CHUNK

            PER_CHUNK = 4 + 2 * (2 + 1 + 2)

            def stats(a, u, o, eps, step, step_count, wait_step):
                for b in range(XC):
                    ins = dve.bn_stats(stat(u)[:, b, o:o + 6], a[:, b, :])
                n_before = step_count()
                ins.then_inc(chain_v, 1)
                wait_step(n_before)
                dve.sem_inc(settled_v, 1)
                for b in range(XC):
                    ins = dve.bn_aggr(stat(u)[:, b, o + 6:o + 8], stat(u)[:, b, o:o + 6])
                step(ins)
                step(dve.tensor_scalar(stat(u)[:, :, o + 7], stat(u)[:, :, o + 7], eps, None, ALU.add))

            def coefs(u, o, step):
                step(dve.reciprocal(stat(u)[:, :, o + 9], stat(u)[:, :, o + 8]))
                step(dve.scalar_tensor_tensor(stat(u)[:, :, o + 10], stat(u)[:, :, o + 6], -1.0, stat(u)[:, :, o + 9],
                                              ALU.mult, ALU.mult))

            final(0, True, False)
            with dve.Fori(1, NCH // 2 - 1) as i:
                final(i, False, False)
            final(NCH // 2 - 1, False, True)


_INS = ["x", "src", "dst", "L0_gnn_qTrans", "L0_gnn_kTrans", "L0_gnn_vTrans", "L0_gnn_ln_scale", "L0_gnn_ln_bias"]
POOL_CONSTS = 10


def kernel(**inputs):
    import numpy as _np
    import concourse.bacc as _bacc
    from concourse import mybir as _mybir
    from concourse.bass_utils import run_bass_kernel_spmd as _run

    nc = _bacc.Bacc("TRN2", target_bir_lowering=False, num_devices=1)
    arrays, args = {}, []
    for name in _INS:
        a = _np.ascontiguousarray(inputs[name])
        arrays[f"in_{name}"] = a
        args.append(nc.dram_tensor(f"in_{name}", a.shape, _mybir.dt.from_np(a.dtype), kind="ExternalInput").ap())
    args.append(nc.dram_tensor("out_0", (NODES, D), _mybir.dt.float32, kind="ExternalOutput").ap())
    build(nc, *args)
    r = _run(nc, [arrays], core_ids=[0])
    return r.results[0]["out_0"]
```

```python
import concourse.bass as bass
from concourse import mybir
from contextlib import ExitStack

P = 128
NODES, EDGES, D, H = 12500, 400000, 128, 8
HD = D // H
NB = -(-NODES // P)
TAIL = NODES - (NB - 1) * P
ROW = 4096
LOG_ROW, LOG_P = 12, 7
FULL_ROWS = EDGES // ROW
REST = EDGES - FULL_ROWS * ROW
SENT_ROW = FULL_ROWS + 1
BPR = 4
SENT_COLS = BPR * P
PADB = BPR * (P - SENT_ROW)
assert PADB >= NB and P * ROW >= EDGES
LOC_SHIFT, BLK_SHIFT = 14, 22
KEY_BASE = 1 << 29
SENT_BIT = 1 << LOC_SHIFT
NO_BLOCK = P - 1
G = 4
FULL = (EDGES + NB * (P - 1)) // P
TILES = -(-FULL // (4 * G)) * 4 * G
QUADS = TILES // G
ITERS = QUADS // 4
WD = D + H
KV = 2 * D
ORDER = [0, 4, 1, 5, 2, 6, 3, 7]
CH = 512
XC = 7
NCH = NB // XC
assert NCH * XC == NB


def flat(t, part_elems, off, dims, rows=P):
    dims = [d for d in dims if d[1] > 1] or [[1, 1]]
    return bass.AP(t, off, [[part_elems, rows]] + dims)


def bcast(v):
    return bass.AP(v.tensor, v.offset, [[0, P], [1, D]])


def build(nc, x, src, dst, wq, wk, wv, ln_scale, ln_bias, out):
    f32, bf16, i32 = mybir.dt.float32, mybir.dt.bfloat16, mybir.dt.int32
    ALU, ACT, AX = mybir.AluOpType, mybir.ActivationFunctionType, mybir.AxisListType
    ET = mybir.EngineType
    ctx = ExitStack()
    with ctx:
        def sb(name, shape, dt):
            return ctx.enter_context(nc.sbuf_tensor(name, shape, dt))

        def sem(name):
            return ctx.enter_context(nc.semaphore(name))

        kv_dram = nc.dram_tensor("kv_rows", [NB * P, KV], f32, kind="Internal").ap()

        q_nodes = sb("q_nodes", [P, NB * D], f32)
        acc = sb("acc", [P, NB * WD], f32)
        keys = sb("keys", [P, 2 * ROW], f32)
        blk_pack = sb("blk_pack", [1, QUADS], i32)
        kv = sb("kv", [P, 4, G, KV], f32)
        prod = sb("prod", [P, G * D], f32)
        wgt = sb("wgt", [P, 2, G, WD], f32)
        onehot = sb("onehot", [P, 4, G * P], bf16)
        onehot32 = sb("onehot32", [P, 2, G * P], f32)
        onehotT = sb("onehotT", [P, 2, G * P], f32)
        att = sb("att", [P, 2, G * H], f32)
        ring = sb("ring", [P, 4, 2, G], i32)
        ident = sb("ident", [P, P], f32)
        ident16 = sb("ident16", [P, P], bf16)
        iota16 = sb("iota16", [P, P], bf16)
        ones = sb("ones", [P, P], f32)
        w_all = sb("w_all", [P, 3 * D], f32)
        xT = sb("xT", [P, 2, P], f32)
        x_tail = sb("x_tail", [P, D], f32)
        part_no = sb("part_no", [P, 1], i32)
        key_const = sb("key_const", [P, 1], i32)
        sign_i = sb("sign_i", [P, LOG_P], i32)
        sign = sb("sign", [P, LOG_P], f32)
        blk_base = sb("blk_base", [P, 1], f32)
        last_step = sb("last_step", [P, 1], f32)
        small_i = sb("small_i", [P, 2], i32)

        src_in = acc[:, 0:ROW].bitcast(i32)
        dst_in = acc[:, ROW:2 * ROW].bitcast(i32)
        E2 = EDGES // P
        src_cnt = acc[:, 2 * ROW:2 * ROW + E2].bitcast(i32)
        junk = acc[:, 2 * ROW + E2:2 * ROW + E2 + (E2 + 1) // 2].bitcast(bf16)
        assert 2 * ROW + E2 + (E2 + 1) // 2 <= NB * WD
        xs = kv[:, :, :, :].rearrange("p a b c -> p (a b c)")[:, 0:2 * XC * D].rearrange("p (s b d) -> p s b d", s=2, b=XC)
        kv_out_buf = wgt[:, :, :, :].rearrange("p a b c -> p (a b c)")[:, 0:2 * KV].rearrange("p (s c) -> p s c", s=2)
        cnt = onehot32[:, 1, 0:NB + 1]
        thr = onehot32[:, 1, P:P + NB + 1]
        mask = onehot[:, :, :].rearrange("p a b -> p (a b)").bitcast(f32)[:, 0:BPR * PADB].rearrange("p (i b) -> p i b", i=BPR)
        cnt_f = prod[:, 0:P]
        cnt_i = prod[:, P:2 * P].bitcast(i32)
        pad = onehot32[:, 1, 2 * P:2 * P + PADB]
        padsel = onehotT[:, :, :].rearrange("p a b -> p (a b)")[:, 0:BPR * PADB].rearrange("p (i b) -> p i b", i=BPR)
        cut = att[:, 0, 0:BPR]
        cut_raw = att[:, 0, BPR:2 * BPR]
        kv_flat = kv[:, :, :, :].rearrange("p a b c -> p (a b c)")
        blk_row = kv_flat[0:1, 0:TILES].bitcast(i32)
        s_rank = kv_flat[:, 2 * XC * D:2 * XC * D + 2 * SENT_COLS]
        s_val = kv_flat[:, 2 * XC * D + 2 * SENT_COLS:2 * XC * D + 4 * SENT_COLS]
        s_step = onehot32[:, :, :].rearrange("p a b -> p (a b)")
        assert 2 * XC * D + 4 * SENT_COLS <= 4 * G * KV and 2 * SENT_COLS <= 2 * G * P

        psum = ctx.enter_context(nc.psum_tensor("psum", [P, 8 * CH], f32))

        def bank(n):
            return psum[:, n * CH:(n + 1) * CH]

        consts = sem("consts")
        const_v = sem("const_v")
        fill = sem("fill")
        src_in_s, dst_in_s, cnt_in_s = sem("src_loaded"), sem("dst_loaded"), sem("cnt_loaded")
        w_in, tail_in = sem("w_loaded"), sem("x_tail_loaded")
        x_in = [sem("x_loaded_0"), sem("x_loaded_1")]
        settled_p, settled_v = sem("settled_pool"), sem("settled_dve")
        chain_v = sem("dve_step")
        chain_p = sem("pool_step")
        counted, totals = sem("counted"), sem("totals")
        cuts_ready, sents_ready, sents_in = sem("cuts_ready"), sem("sents_ready"), sem("sents_in")
        sents_free = sem("sentinels_place_free")
        xt_psum, xt_sb, proj, qkv_sb, q_stored = (sem(n) for n in ("xt_psum", "xt_sb", "projected", "kv_in_sbuf", "q_in_sbuf"))
        kv_out = [sem("kv_stored_0"), sem("kv_stored_1")]
        c_sorted, c_flipped, c_moved = sem("chunk_sorted"), sem("chunk_flipped"), sem("chunk_moved")
        decoded = sem("decoded")
        acc_zero = sem("acc_zero")
        ring_ready, oh_ready, t_ready, ohT_ready, oh32_ready = (sem(n) for n in ("ring_ready", "onehot_ready", "transposed", "onehotT_ready", "onehot32_ready"))
        q_ready, seg_ready, exp_ready = sem("q_gathered"), sem("seg_summed"), sem("exp_ready")
        att_done, w_done, acc_done = sem("att_clipped"), sem("weighted"), sem("accumulated")
        gathered = [sem(f"kv_gathered_{n}") for n in range(4)]
        xf_in = [sem(f"x_again_{n}") for n in range(4)]
        sc_in = sem("scale_loaded")
        stored = [sem(f"out_stored_{n}") for n in range(4)]
        chain_1, chain_2 = sem("first_norm_step"), sem("second_norm_step")
        var1, std1, coef1, norm1, res2, var2, std2, coef2, norm2 = (sem(n) for n in (
            "var1", "std1", "coef1", "norm1", "res2", "var2", "std2", "coef2", "norm2"))
        block = ctx.enter_context(nc.Block())

        def side(buf):
            return buf * ROW

        NTR = 2 * LOG_P + 1

        def plan():
            steps = [("rows", k, j) for k in range(1, LOG_ROW + 1) for j in range(k - 1, -1, -1)]
            n = 0
            for k in range(LOG_ROW + 1, LOG_ROW + LOG_P + 1):
                steps.append(("flip", n, k))
                steps += [("cols", k, j) for j in range(k - 1, LOG_ROW - 1, -1)]
                steps.append(("flip", n + 1, k))
                least = LOG_P if k == LOG_ROW + LOG_P else 0
                steps += [("rows", k, j) for j in range(LOG_ROW - 1, least - 1, -1)]
                n += 2
            steps.append(("flip", n, 0))
            return steps

        PLAN = plan()

        def buffers():
            at, found = 0, []
            for kind, _, _ in PLAN:
                found.append(at)
                at = 1 - at
            return found + [at]

        BUF = buffers()
        FLIPS = [(s, PLAN[s][1], PLAN[s][2]) for s in range(len(PLAN)) if PLAN[s][0] == "flip"]
        assert len(FLIPS) == NTR
        CUTS_AT = PLAN.index(("rows", LOG_ROW, 10))
        SENTS_AT = PLAN.index(("rows", LOG_ROW, 2))
        SENT_BUF = BUF[SENTS_AT + 1]
        END = BUF[-1]
        IDX = 1 - END
        tiles_i = keys[:, side(END):side(END) + TILES].bitcast(i32)
        idx_i = keys[:, side(IDX):side(IDX) + TILES].bitcast(i32)

        def quad_columns(q):
            both = keys[:, :].bitcast(i32).rearrange("p (two c) -> p two c", two=2)
            return both[:, :, bass.ds(q * G, G)]

        FIRST_IS_IDX = IDX == 0
        R_IDX, R_LOC = (0, 1) if FIRST_IS_IDX else (1, 0)

        def seg(j, t):
            return bank(4 + 2 * (j % 2) + t // 2)[:, (t % 2) * WD:(t % 2 + 1) * WD]

        CLAMPED = "each packed block is the minimum of itself and NB - 1, taken on the chip"

        def packed_blocks(engine, first_quad, n):
            return nc.values_load_multi_w_load_instructions(blk_pack[0:1, bass.ds(first_quad, n)], engines=(engine,),
                                                            min_val=0, max_val=(1 << G * LOG_P) - 1,
                                                            skip_runtime_bounds_check_because=CLAMPED)[1]

        def places(packed, width):
            fields = [(packed >> (LOG_P * t)) & (P - 1) if t < G - 1 else packed >> (LOG_P * t) for t in range(G)]
            return [nc.snap(nc.s_assert_within(f, 0, NB - 1, skip_runtime_bounds_check_because=CLAMPED) * width)
                    for f in fields]

        FIN = NCH
        SLOT = ROW // 2

        def res(u):
            return keys[:, u * SLOT:u * SLOT + XC * D].rearrange("p (b d) -> p b d", b=XC)

        def res_b(u):
            return keys[:, u * SLOT + XC * D:u * SLOT + 2 * XC * D].rearrange("p (b d) -> p b d", b=XC)

        STAT = 21
        assert 2 * XC * D + XC * STAT <= SLOT

        def stat(u):
            return keys[:, u * SLOT + 2 * XC * D:u * SLOT + 2 * XC * D + XC * STAT].rearrange("p (b s) -> p b s", b=XC)

        xs4 = kv_flat[:, 0:4 * XC * D].rearrange("p (s b d) -> p s b d", s=4, b=XC)

        scale_bc = prod[:, 0:D]
        bias_bc = prod[:, D:2 * D]

        @block.sync
        def _(sp):
            sp.wait_ge(fill, 2)
            for t, flat_in, done in ((src, src_in, src_in_s), (dst, dst_in, dst_in_s)):
                a = (FULL_ROWS // 16) * 16
                sp.dma_start(flat_in[0:a, :], t[0:a * ROW].rearrange("(p c) -> p c", c=ROW)).then_inc(done, 16)
                sp.dma_start(flat_in[a:FULL_ROWS, :], t[a * ROW:FULL_ROWS * ROW].rearrange("(p c) -> p c", c=ROW)).then_inc(done, 16)
                sp.dma_start(flat_in[FULL_ROWS:FULL_ROWS + 1, 0:REST], t[FULL_ROWS * ROW:EDGES].rearrange("(p c) -> p c", p=1)).then_inc(done, 16)
                if t is src:
                    sp.dma_start(src_cnt, src.rearrange("(p c) -> p c", p=P)).then_inc(cnt_in_s, 16)
            for n, w in enumerate((wq, wk, wv)):
                sp.dma_start(w_all[:, n * D:(n + 1) * D], w).then_inc(w_in, 16)
            sp.wait_ge(consts, 1)
            sp.dma_start(x_tail[0:TAIL, :], x[(NB - 1) * P:NODES, :]).then_inc(tail_in, 16)

            def load_x(c, nblocks, into, slot, done):
                rows = x[bass.ds(c * XC * P, nblocks * P), :]
                sp.dma_start(into[:, slot, 0:nblocks, :], rows.rearrange("(b p) d -> p b d", p=P)).then_inc(done, 16)

            load_x(0, XC, xs, 0, x_in[0])
            load_x(1, XC, xs, 1, x_in[1])

            def prep(i, last, before_last):
                for u in range(2 * XC):
                    b = i * (2 * XC) + u
                    sp.wait_ge(qkv_sb, b + 1)
                    sp.dma_start(kv_dram[bass.ds(b * P, P), :], kv_out_buf[:, u % 2, :]).then_inc(kv_out[u % 2], 16)
                    if u % XC == XC - 1 and not last:
                        c = 2 * i + (2 if u < XC else 3)
                        sp.wait_ge(xt_psum, b + 1)
                        n = XC - 1 if before_last and u >= XC else XC
                        load_x(c, n, xs, u // XC, x_in[u // XC])

            sp.wait_ge(sents_ready, 1)
            sp.wait_ge(sents_free, 1)
            ends = keys[SENT_ROW:P, side(SENT_BUF):side(SENT_BUF) + ROW]
            sp.dma_start(ends[:, 0:SENT_COLS], s_val[SENT_ROW:P, 0:SENT_COLS]).then_inc(sents_in, 16)
            sp.dma_start(ends[:, ROW - SENT_COLS:ROW], s_val[SENT_ROW:P, SENT_COLS:2 * SENT_COLS]).then_inc(sents_in, 16)
            with sp.Fori(0, NCH // 2 - 2) as i:
                prep(i, False, False)
            prep(NCH // 2 - 2, False, True)
            prep(NCH // 2 - 1, True, False)

            sp.wait_ge(w_done, QUADS)
            sp.dma_start(scale_bc, bcast(ln_scale)).then_inc(sc_in, 16)
            sp.dma_start(bias_bc, bcast(ln_bias)).then_inc(sc_in, 16)

            def load_again(c, u, full, old):
                if old:
                    sp.wait_ge(res2, c - 3)
                rows = XC if full else XC - 1
                load_x(c, rows, xs4, u, xf_in[u])
                if not full:
                    sp.dma_start(xs4[0:TAIL, u, XC - 1, :], x[(NB - 1) * P:NODES, :]).then_inc(xf_in[u], 16)

            def store(c, u, full):
                sp.wait_ge(norm2, c + 1)
                rows = XC if full else XC - 1
                to = out[bass.ds(c * XC * P, rows * P), :]
                sp.dma_start(to.rearrange("(b p) d -> p b d", p=P), res(u)[:, 0:rows, :]).then_inc(stored[u], 16)
                if not full:
                    sp.dma_start(out[(NB - 1) * P:NODES, :], res(u)[0:TAIL, XC - 1, :]).then_inc(stored[u], 16)

            for c in range(4):
                load_again(c, c, True, False)
            with sp.Fori(0, FIN // 4 - 1) as i:
                for u in range(4):
                    store(i * 4 + u, u, True)
                    load_again(i * 4 + 4 + u, u, True, True)
            for c in range(4 * (FIN // 4 - 1), FIN):
                store(c, c % 4, c < FIN - 1)
                if c + 4 < FIN:
                    load_again(c + 4, c % 4, c + 4 < FIN - 1, True)
            for u in range(4):
                sp.wait_ge(stored[u], 16 * len(range(u, FIN, 4)) + (16 if (FIN - 1) % 4 == u else 0))

        @block.gpsimd
        def _(pool):
            steps = [0]

            def link(ins):
                steps[0] += 1
                ins.then_inc(chain_p, 1)
                pool.wait_ge(chain_p, steps[0])

            pool.memset(src_in[96:P, :], NO_BLOCK * P).then_inc(fill, 1)
            pool.wait_ge(fill, 1)
            pool.memset(dst_in[96:P, :], SENT_BIT).then_inc(fill, 1)
            pool.wait_ge(fill, 2)
            pool.memset(x_tail[:, :], 0.0).then_inc(consts, 1)
            pool.wait_ge(consts, 1)
            link(pool.iota(part_no[:, :], [[0, 1]], base=0, channel_multiplier=1))
            pool.memset(pad, 0.0).then_inc(consts, 1)
            pool.wait_ge(consts, 2)
            link(pool.memset(ident[:, :], 0.0))
            link(pool.memset(ones[:, :], 1.0))
            link(pool.affine_select(out=ident[:, :], in_=ident[:, :], compare_op=ALU.not_equal, fill=1.0, base=0,
                                    pattern=[[-1, P]], channel_multiplier=1))
            link(pool.tensor_copy(ident16[:, :], ident[:, :]))
            link(pool.iota(cnt_i[:, 0:P], [[2, P]], base=0, channel_multiplier=0))
            link(pool.tensor_copy(iota16[:, :], cnt_i[:, 0:P]))
            link(pool.iota(cnt_i[:, 0:NB + 1], [[-P, NB + 1]], base=0, channel_multiplier=0))
            link(pool.tensor_copy(thr, cnt_i[:, 0:NB + 1]))
            link(pool.tensor_scalar(thr, thr, 0.5, None, ALU.add))
            link(pool.memset(cnt[:, 0:1], float(E2)))
            link(pool.memset(cnt[:, NB:NB + 1], float(-E2)))
            for i in range(BPR):
                link(pool.memset(mask[:, i, :], 1.0))
                link(pool.affine_select(out=mask[:, i, :], in_=mask[:, i, :], compare_op=ALU.is_equal, fill=0.0,
                                        base=BPR * SENT_ROW - i, pattern=[[1, PADB]], channel_multiplier=-BPR))
            link(pool.iota(small_i[:, 0:1], [[0, 1]], base=-BPR * SENT_ROW, channel_multiplier=BPR))
            link(pool.iota(small_i[:, 1:2], [[0, 1]], base=NO_BLOCK - (BPR - 1) + BPR * SENT_ROW, channel_multiplier=-BPR))
            link(pool.tensor_copy(blk_base[:, :], small_i[:, 0:1]))
            pool.tensor_copy(last_step[:, :], small_i[:, 1:2]).then_inc(consts, 1)
            pool.wait_ge(consts, 3)

            def settle():
                pool.sem_inc(settled_p, 1)

            lo = 96
            rank, val = s_rank[lo:P, :], s_val[lo:P, :]
            left, right = (s_val[lo:P, h * SENT_COLS:(h + 1) * SENT_COLS] for h in range(2))
            link(pool.iota(left.bitcast(i32), [[1, SENT_COLS]], base=SENT_COLS, channel_multiplier=0))
            link(pool.iota(right.bitcast(i32), [[-1, SENT_COLS]], base=2 * SENT_COLS - 1, channel_multiplier=0))
            link(pool.tensor_copy(rank, val.bitcast(i32)))
            pool.wait_ge(const_v, 1)
            for h in range(2):
                side_sign = sign[lo:P, 0:1]
                half = s_rank[lo:P, h * SENT_COLS:(h + 1) * SENT_COLS]
                link(pool.tensor_scalar(s_step[lo:P, 0:1], side_sign, float(-SENT_COLS if h == 0 else SENT_COLS), None, ALU.mult))
                link(pool.tensor_scalar(half, half, s_step[lo:P, 0:1], None, ALU.add))
            pool.wait_ge(cuts_ready, 1)
            link(pool.tensor_scalar(val, rank, cut[lo:P, 0:1], blk_base[lo:P, :], ALU.is_ge, ALU.add))
            link(pool.tensor_scalar(s_step[lo:P, :], rank, cut[lo:P, 1:2], None, ALU.is_ge))
            link(pool.tensor_tensor(val, val, s_step[lo:P, :], ALU.add))
            link(pool.tensor_scalar(s_step[lo:P, :], rank, cut[lo:P, 2:3], None, ALU.is_ge))
            link(pool.tensor_tensor(val, val, s_step[lo:P, :], ALU.add))
            link(pool.tensor_scalar(s_step[lo:P, :], rank, cut[lo:P, 3:4], last_step[lo:P, :], ALU.is_ge, ALU.mult))
            link(pool.tensor_tensor(val, val, s_step[lo:P, :], ALU.add))
            link(pool.tensor_scalar(rank.bitcast(i32), val, float(1 << BLK_SHIFT), float(KEY_BASE + SENT_BIT), ALU.mult, ALU.add))
            pool.tensor_scalar(val, rank, sign[lo:P, 0:1], None, ALU.mult).then_inc(sents_ready, 1)
            pool.wait_ge(sents_ready, 1)

            pool.memset(acc[:, :], 0.0).then_inc(acc_zero, 1)
            pool.wait_ge(acc_zero, 1)
            base = steps[0]

            for s in range(2):
                pool.wait_ge(kv_out[s], 16 * (NB // 2))

            def gather(i, first):
                for j in range(4):
                    q = i * 4 + j
                    pool.wait_ge(ring_ready, q + 1)
                    if not first:
                        pool.wait_ge(w_done, q - 3)
                    settle()
                    for t in range(G):
                        pool.indirect_dma_start(kv[:, j, t, :], None, kv_dram,
                                                bass.IndirectOffsetOnAxis(ap=ring[:, j, R_IDX, t:t + 1], axis=0)
                                                ).then_inc(gathered[j], 16)

            gather(0, True)
            with pool.Fori(1, ITERS) as i:
                gather(i, False)

            pool.wait_ge(sc_in, 32)

            def bc(v, n=XC):
                return v.unsqueeze(1).to_broadcast([P, n, D])

            def final(i, slots):
                for u in range(slots):
                    c = 4 * i + u
                    n = c * 2 + total_split
                    pool.wait_ge(norm1, c + 1)
                    pool.tensor_tensor(res_b(u), res_b(u), bc(scale_bc), ALU.mult).then_inc(chain_p, 1)
                    pool.wait_ge(chain_p, n + 1)
                    pool.tensor_tensor(res_b(u), res_b(u), bc(bias_bc), ALU.add).then_inc(chain_p, 1)
                    pool.wait_ge(chain_p, n + 2)
                    pool.tensor_tensor(res_b(u), res_b(u), xs4[:, u, :, :], ALU.add).then_inc(res2, 1)

            total_split = base
            with pool.Fori(0, FIN // 4) as i:
                final(i, 4)
            final(FIN // 4, FIN % 4)

        @block.scalar
        def _(act):
            act.wait_ge(chain_p, POOL_CONSTS)
            act.wait_ge(cnt_in_s, 16)

            def count(t):
                act.activation(junk[:, 0:E2], src_cnt, ACT.Sign, bias=thr[:, bass.ds(t, 1)], scale=1.0,
                               accum_out=cnt[:, bass.ds(t, 1)]).then_inc(counted, 1)
                act.wait_ge(counted, t)

            with act.Fori(0, (NB - 1) // 12) as i:
                for u in range(12):
                    count(i * 12 + (u + 1))
            for t in range((NB - 1) // 12 * 12 + 1, NB):
                count(t)

            def pair(g, u, first):
                b0 = g * (2 * XC) + 2 * u
                for h in range(2):
                    act.wait_ge(xt_psum, b0 + h + 1)
                    if not first:
                        act.wait_ge(proj, b0 + h - 1)
                    act.activation(xT[:, h, :], bank(h)[:, 0:P], ACT.Copy).then_inc(xt_sb, 1)
                for h in range(2):
                    act.wait_ge(proj, b0 + h + 1)
                    act.activation(q_nodes[:, bass.ds(b0 * D + h * D, D)], bank(2 + h)[:, 0:D], ACT.Copy).then_inc(q_stored, 1)
                    if not first:
                        act.wait_ge(kv_out[h], (u + g * XC) * 16)
                    act.activation(kv_out_buf[:, h, :], bank(2 + h)[:, D:3 * D], ACT.Copy).then_inc(qkv_sb, 1)

            def project(g):
                if g == 0:
                    pair(0, 0, True)
                with act.Fori(1 if g == 0 else 0, XC) as u:
                    pair(g, u, False)

            for s, n, k in FLIPS:
                to = side(BUF[s + 1])
                into_rows = n % 2 == 1
                if n == NTR - 1:
                    act.wait_ge(c_flipped, 8 * NTR)
                for pos, c in enumerate(ORDER):
                    act.wait_ge(c_flipped, 8 * n + pos + 1)
                    if n == NTR - 1:
                        gs = CH // P
                        view = keys[:, to:to + ROW].rearrange("p (a g) -> p g a", g=ROW // P)[:, c * gs:(c + 1) * gs, :]
                        act.activation(view, bank(pos).rearrange("p (g a) -> p g a", g=gs), ACT.Copy).then_inc(c_moved, 1)
                    else:
                        signed = into_rows and k < LOG_ROW + LOG_P
                        sc = sign[:, k - LOG_ROW:k - LOG_ROW + 1] if signed else 1.0
                        act.activation(keys[:, to + c * CH:to + (c + 1) * CH], bank(pos), ACT.Copy, scale=sc).then_inc(c_moved, 1)
                if n % 2 == 1:
                    project(n // 2)

            act.wait_ge(decoded, 1)

            def copy_ring(q, j, gathers):
                if gathers is not None:
                    act.wait_ge(gathered[j], gathers)
                    act.wait_ge(oh_ready, q - 3)
                act.activation(ring[:, j, :, :], quad_columns(q), ACT.Copy).then_inc(ring_ready, 1)

            def expand(q, j, first2):
                act.wait_ge(oh_ready, q + 1)
                if not first2:
                    act.wait_ge(seg_ready, q - 1)
                act.activation(onehot32[:, j % 2, :], onehot[:, j % 4, :], ACT.Copy).then_inc(oh32_ready, 1)

            def exps(q, j, first2):
                act.wait_ge(att_done, q + 1)
                if not first2:
                    act.wait_ge(seg_ready, q - 1)
                a = att[:, j % 2, :].rearrange("p (g h) -> p g h", g=G)
                act.activation(wgt[:, j % 2, :, D:WD], a, ACT.Exp).then_inc(exp_ready, 1)

            def move_T(q, j, first2):
                act.wait_ge(t_ready, q + 1)
                if not first2:
                    act.wait_ge(q_ready, q - 1)
                act.activation(onehotT[:, j % 2, :], bank(j % 2)[:, 0:CH // 2].bitcast(bf16), ACT.Copy).then_inc(ohT_ready, 1)

            for q in range(4):
                copy_ring(q, q, None)
            for q in range(3):
                move_T(q, q, q < 2)
            exps(0, 0, True)

            def steps(i, first, last):
                for j in range(4):
                    s = i * 4 + j
                    if not last:
                        copy_ring(s + 4, j, i * (16 * G) + 16 * G)
                    expand(s, j, first and j < 2)
                    if not (last and j == 3):
                        exps(s + 1, j + 1, first and j == 0)
                    if not (last and j >= 1):
                        move_T(s + 3, j + 3, False)

            steps(0, True, False)
            with act.Fori(1, ITERS - 1) as i:
                steps(i, False, False)
            steps(ITERS - 1, False, True)

            def root(u, o, var, std, c):
                act.wait_ge(var, c + 1)
                act.activation(stat(u)[:, :, o + 2], stat(u)[:, :, o + 1], ACT.Sqrt).then_inc(std, 1)

            def normalise(u, o, coef, norm, c, a, b):
                act.wait_ge(coef, c + 1)
                for k in range(XC):
                    ins = act.activation(b[:, k, :], a[:, k, :], ACT.Identity, scale=stat(u)[:, k, o + 3:o + 4],
                                         bias=stat(u)[:, k, o + 4:o + 5])
                ins.then_inc(norm, 1)

            def final(i, slots, old, new):
                for u in range(slots):
                    c, v = 4 * i + u, (u + 2) % 4
                    if new:
                        root(u, 6, var1, std1, c)
                    if old or u >= 2:
                        root(v, 16, var2, std2, c - 2)
                    if new:
                        normalise(u, 6, coef1, norm1, c, res(u), res_b(u))
                    if old or u >= 2:
                        normalise(v, 16, coef2, norm2, c - 2, res_b(v), res(v))

            final(0, 4, False, True)
            with act.Fori(1, FIN // 4) as i:
                final(i, 4, True, True)
            final(FIN // 4, 2, True, True)
            for c in (FIN, FIN + 1):
                v = (c - 2) % 4
                root(v, 16, var2, std2, c - 2)
                normalise(v, 16, coef2, norm2, c - 2, res_b(v), res(v))

        @block.tensor
        def _(pe):
            pe.wait_ge(consts, 3)
            pe.wait_ge(counted, NB - 1)
            pe.matmul(bank(4)[:, 0:NB + 1], ones[:, :], cnt, start=True, stop=True).then_inc(totals, 1)
            pe.wait_ge(w_in, 48)
            pe.wait_ge(tail_in, 16)

            def pair(g, u, first, last):
                b0 = g * (2 * XC) + 2 * u
                x14 = kv_flat[:, 0:2 * XC * D]
                for h in range(2):
                    if not first:
                        pe.wait_ge(xt_sb, b0 + h - 1)
                    x_b = x_tail[:, :] if last and h == 1 else x14[:, (2 * u + h) * D:(2 * u + h + 1) * D]
                    pe.transpose(bank(h)[:, 0:P], x_b, ident[:, :]).then_inc(xt_psum, 1)
                for h in range(2):
                    pe.wait_ge(xt_sb, b0 + h + 1)
                    if not first:
                        pe.wait_ge(qkv_sb, b0 + h - 1)
                    pe.matmul(bank(2 + h)[:, 0:3 * D], xT[:, h, :], w_all[:, :], start=True, stop=True).then_inc(proj, 1)

            def project(g):
                pe.wait_ge(x_in[0], 16 * g + 16)
                pe.wait_ge(x_in[1], 16 * g + 16)
                for u in range(XC):
                    pair(g, u, g + u == 0, g == NCH // 2 - 1 and u == XC - 1)
                pe.wait_ge(qkv_sb, (g + 1) * 2 * XC)

            for s, n, k in FLIPS:
                at = side(BUF[s])
                for pos, c in enumerate(ORDER):
                    pe.wait_ge(c_sorted, 8 * n + pos + 1)
                    if n:
                        pe.wait_ge(c_moved, 8 * (n - 1) + pos + 1)
                    for g in range(CH // P):
                        o = c * CH + g * P
                        ins = pe.transpose(bank(pos)[:, g * P:(g + 1) * P], keys[:, at + o:at + o + P], ident[:, :])
                    ins.then_inc(c_flipped, 1)
                if n % 2 == 1:
                    pe.wait_ge(c_moved, 8 * (n + 1))
                    project(n // 2)
            pe.wait_ge(c_moved, 8 * NTR)
            pe.wait_ge(q_stored, NB)
            pe.wait_ge(decoded, 1)

            def transposes(q, j, first2):
                pe.wait_ge(oh_ready, q + 1)
                if not first2:
                    pe.wait_ge(ohT_ready, q - 1)
                for t in range(G):
                    ins = pe.transpose(bank(j % 2)[:, t * P // 2:(t + 1) * P // 2].bitcast(bf16),
                                       onehot[:, j % 4, t * P:(t + 1) * P], ident16[:, :])
                ins.then_inc(t_ready, 1)

            def gather_q(q, j, packed, first2):
                at = places(packed, D)
                pe.wait_ge(ohT_ready, q + 1)
                if not first2:
                    pe.wait_ge(att_done, q - 1)
                for t in range(G):
                    ins = pe.matmul(bank(2 + j % 2)[:, t * D:(t + 1) * D], onehotT[:, j % 2, t * P:(t + 1) * P],
                                    q_nodes[:, bass.ds(at[t], D)], start=True, stop=True)
                ins.then_inc(q_ready, 1)

            def segment_sum(q, j, first2):
                pe.wait_ge(w_done, q + 1)
                pe.wait_ge(oh32_ready, q + 1)
                if not first2:
                    pe.wait_ge(acc_done, (q - 1) * G)
                for t in range(G):
                    ins = pe.matmul(seg(j, t), onehot32[:, j % 2, t * P:(t + 1) * P], wgt[:, j % 2, t, :], start=True, stop=True)
                ins.then_inc(seg_ready, 1)

            early = packed_blocks(ET.PE, 0, 2)
            for q in range(3):
                transposes(q, q, q < 2)
                if q < 2:
                    gather_q(q, q, early[q], True)

            def steps(i, first, last):
                later = packed_blocks(ET.PE, i * 4 + 2, 2 if last else 4)
                for j in range(4):
                    s = i * 4 + j
                    if not (last and j >= 2):
                        gather_q(s + 2, j + 2, later[j], False)
                    if not (last and j >= 1):
                        transposes(s + 3, j + 3, False)
                    if not (first and j == 0):
                        segment_sum(s - 1, j + 3, first and j <= 2)

            steps(0, True, False)
            with pe.Fori(1, ITERS - 1) as i:
                steps(i, False, False)
            steps(ITERS - 1, False, True)
            segment_sum(QUADS - 1, 3, False)

        @block.vector
        def _(dve):
            steps_v = [0]

            def link(ins):
                steps_v[0] += 1
                ins.then_inc(chain_v, 1)
                dve.wait_ge(chain_v, steps_v[0])

            dve.wait_ge(chain_p, 1)
            for m in range(LOG_P):
                link(dve.tensor_scalar(sign_i[:, m:m + 1], part_no[:, :], m, 1, ALU.logical_shift_right, ALU.bitwise_and))
            dve.tensor_scalar(sign[:, :], sign_i[:, :], -2.0, 1.0, ALU.mult, ALU.add).then_inc(const_v, 1)
            dve.wait_ge(const_v, 1)
            link(dve.tensor_scalar(key_const[:, :], part_no[:, :], 31, KEY_BASE, ALU.logical_shift_left, ALU.bitwise_or))

            first = keys[:, side(BUF[0]):side(BUF[0]) + ROW].bitcast(i32)
            other = keys[:, side(1 - BUF[0]):side(1 - BUF[0]) + ROW].bitcast(i32)
            dve.wait_ge(src_in_s, 48)
            link(dve.tensor_scalar(other, src_in, LOC_SHIFT + 1, key_const[:, 0:1], ALU.logical_shift_left, ALU.bitwise_or))
            dve.wait_ge(dst_in_s, 48)
            link(dve.tensor_tensor(first, other, dst_in, ALU.bitwise_or))

            def exchange(to, at, k, j, negated=False, c=None, rows=P):
                o = 0 if c is None else c * CH
                n = ROW if c is None else CH
                if k is None:
                    dims = mins = maxs = [[2 << j, n >> (j + 1)], [1, 1 << j]]
                else:
                    rest = [[2 << j, 1 << (k - 1 - j)], [1, 1 << j]]
                    hi = [2 << k, n >> (k + 1)]
                    dims = [hi, [1 << k, 2]] + rest
                    mins = [hi, [(1 << k) + (1 << j), 2]] + rest
                    maxs = [hi, [(1 << k) - (1 << j), 2]] + rest
                if k is not None and n >> (k + 1) > 1 and k - 1 - j > 0 and j > 0:
                    for r, first_op, second_op in ((0, ALU.min, ALU.max), (1 << k, ALU.max, ALU.min)):
                        own = [hi] + rest
                        a, b = (flat(keys, 2 * ROW, at + o + r + h, own, rows) for h in (0, 1 << j))
                        dve.tensor_tensor(flat(keys, 2 * ROW, to + o + r, own, rows), a, b, first_op)
                        ins = dve.tensor_tensor(flat(keys, 2 * ROW, to + o + r + (1 << j), own, rows), a, b, second_op)
                    return ins
                a = flat(keys, 2 * ROW, at + o, dims, rows)
                b = flat(keys, 2 * ROW, at + o + (1 << j), dims, rows)
                low = flat(keys, 2 * ROW, to + o, mins, rows)
                high = flat(keys, 2 * ROW, to + o + (1 << j), maxs, rows)
                if negated:
                    runs = [(0, ALU.min, ALU.max)] if k is None else [(0, ALU.min, ALU.max), (1 << k, ALU.max, ALU.min)]
                    for r, first_op, second_op in runs:
                        ab = [[2 << j, n >> (j + 1)] if k is None else [2 << k, n >> (k + 1)], [1, 1 << j]]
                        lo_at, lo_to = at + o + r, to + o + r
                        a, b = (flat(keys, 2 * ROW, lo_at + h, ab) for h in (0, 1 << j))
                        dve.scalar_tensor_tensor(flat(keys, 2 * ROW, lo_to, ab), b, -1.0, a, ALU.mult, first_op)
                        ins = dve.scalar_tensor_tensor(flat(keys, 2 * ROW, lo_to + (1 << j), ab), b, -1.0, a, ALU.mult, second_op)
                    return ins
                dve.tensor_tensor(low, a, b, ALU.min)
                return dve.tensor_tensor(high, a, b, ALU.max)

            def exchange_halves(to, at, c):
                a, b = (keys[:, at + h + c * CH:at + h + (c + 1) * CH] for h in (0, ROW // 2))
                dve.tensor_tensor(keys[:, to + c * CH:to + (c + 1) * CH], a, b, ALU.min)
                return dve.tensor_tensor(keys[:, to + ROW // 2 + c * CH:to + ROW // 2 + (c + 1) * CH], a, b, ALU.max)

            def cut_rows():
                dve.wait_ge(totals, 1)
                dve.wait_ge(consts, 3)
                tot = padsel.rearrange("p i b -> p (i b)")[:, 0:NB + 1]
                link(dve.tensor_copy(tot, bank(4)[:, 0:NB + 1]))
                link(dve.tensor_tensor(cnt_f[:, 0:NB], tot[:, 0:NB], tot[:, 1:NB + 1], ALU.subtract))
                link(dve.tensor_scalar(cnt_i[:, 0:NB], cnt_f[:, 0:NB], 0.5, None, ALU.mult))
                link(dve.tensor_scalar(cnt_i[:, 0:NB], cnt_i[:, 0:NB], P - 1, None, ALU.bitwise_and))
                link(dve.tensor_scalar(cnt_i[:, 0:NB], cnt_i[:, 0:NB], -1.0, float(P), ALU.mult, ALU.add))
                link(dve.tensor_scalar(cnt_i[:, 0:NB], cnt_i[:, 0:NB], P - 1, None, ALU.bitwise_and))
                link(dve.tensor_copy(pad[:, 0:NB], cnt_i[:, 0:NB]))
                link(dve.tensor_tensor(padsel, mask, pad.unsqueeze(1).to_broadcast([P, BPR, PADB]), ALU.mult))
                link(dve.tensor_reduce(cut_raw, padsel, AX.X, ALU.add))
                link(dve.tensor_copy(cut[:, 0:1], cut_raw[:, 0:1]))
                for i in range(1, BPR):
                    ins = dve.tensor_tensor(cut[:, i:i + 1], cut[:, i - 1:i], cut_raw[:, i:i + 1], ALU.add)
                    if i < BPR - 1:
                        link(ins)
                ins.then_inc(cuts_ready, 1)

            for s, (kind, k, j) in enumerate(PLAN):
                at, to = side(BUF[s]), side(BUF[s + 1])
                if kind == "flip":
                    continue
                direction = k if kind == "rows" and k < LOG_ROW else None
                jj = j
                if kind == "cols":
                    direction, jj = (k - LOG_ROW if k < LOG_ROW + LOG_P else None), j - LOG_ROW
                before, after = PLAN[s - 1] if s else ("", 0, 0), PLAN[s + 1]
                chunked_in, chunked_out = before[0] == "flip", after[0] == "flip"
                if kind == "rows" and chunked_in:
                    for m in range(4):
                        dve.wait_ge(c_moved, 8 * before[1] + 2 * m + 2)
                        ins = exchange_halves(to, at, m)
                    link(ins)
                elif chunked_in or chunked_out:
                    for pos, c in enumerate(ORDER):
                        if chunked_in:
                            dve.wait_ge(c_moved, 8 * before[1] + pos + 1)
                        ins = exchange(to, at, direction, jj, negated=chunked_in, c=c)
                        if chunked_out:
                            ins.then_inc(c_sorted, 1)
                    if not chunked_out:
                        link(ins)
                elif s == SENTS_AT:
                    dve.nop().then_inc(sents_free, 1)
                    link(exchange(to, at, direction, jj, rows=SENT_ROW))
                    dve.wait_ge(sents_in, 32)
                else:
                    link(exchange(to, at, direction, jj))
                if s == CUTS_AT:
                    cut_rows()

            dve.wait_ge(c_moved, 8 * NTR)
            link(dve.tensor_scalar(blk_row[:, :], tiles_i[0:1, :], BLK_SHIFT, P - 1, ALU.logical_shift_right, ALU.bitwise_and))
            link(dve.tensor_scalar(blk_row[:, :], blk_row[:, :], float(NB - 1), None, ALU.min))
            by_quad = blk_row[:, :].rearrange("p (q g) -> p g q", g=G)
            link(dve.tensor_copy(blk_pack[:, :], by_quad[:, 0, :]))
            for t in range(1, G):
                link(dve.tensor_scalar(by_quad[:, t, :], by_quad[:, t, :], LOG_P * t, None, ALU.logical_shift_left))
                link(dve.tensor_tensor(blk_pack[:, :], blk_pack[:, :], by_quad[:, t, :], ALU.bitwise_or))
            link(dve.tensor_scalar(idx_i, tiles_i, (1 << LOC_SHIFT) - 1, None, ALU.bitwise_and))
            dve.tensor_scalar(tiles_i, tiles_i, LOC_SHIFT, 2 * P - 1, ALU.logical_shift_right, ALU.bitwise_and).then_inc(decoded, 1)
            dve.wait_ge(decoded, 1)
            dve.wait_ge(acc_zero, 1)
            base_v = steps_v[0]

            def onehots(q, j, first):
                dve.wait_ge(ring_ready, q + 1)
                if not first:
                    dve.wait_ge(t_ready, q - 3)
                    dve.wait_ge(oh32_ready, q - 3)
                oh = onehot[:, j % 4, :].rearrange("p (g n) -> p g n", g=G)
                dve.tensor_tensor(oh, iota16[:, :].unsqueeze(1).to_broadcast([P, G, P]),
                                  ring[:, j % 4, R_LOC, :].unsqueeze(2).to_broadcast([P, G, P]), ALU.is_equal
                                  ).then_inc(oh_ready, 1)

            def products(q, j, arrived):
                dve.wait_ge(gathered[j % 4], arrived)
                dve.wait_ge(q_ready, q + 1)
                p = prod[:, :].rearrange("p (g d) -> p g d", g=G)
                ps = bank(2 + j % 2).rearrange("p (g d) -> p g d", g=G)
                dve.tensor_tensor(p, kv[:, j % 4, :, 0:D], ps, ALU.mult).then_inc(chain_v, 1)

            def reduce_heads(q, j):
                dve.wait_ge(chain_v, base_v + 2 * q + 1)
                dve.tensor_reduce(att[:, j % 2, :], prod[:, :].rearrange("p (gh e) -> p gh e", e=HD), AX.X, ALU.add
                                  ).then_inc(chain_v, 1)

            def clip(q, j):
                dve.wait_ge(chain_v, base_v + 2 * q + 2)
                dve.tensor_scalar(att[:, j % 2, :], att[:, j % 2, :], -10.0, 10.0, ALU.max, ALU.min).then_inc(att_done, 1)

            def weight(q, j, first2):
                dve.wait_ge(exp_ready, q + 1)
                w = wgt[:, j % 2, :, 0:D].rearrange("p g (h e) -> p g h e", h=H)
                v = kv[:, j % 4, :, D:KV].rearrange("p g (h e) -> p g h e", h=H)
                e = wgt[:, j % 2, :, D:WD].unsqueeze(3).to_broadcast([P, G, H, HD])
                dve.tensor_tensor(w, v, e, ALU.mult).then_inc(w_done, 1)

            def accumulate(q, j, t, at, first):
                if t == 0:
                    dve.wait_ge(seg_ready, q + 1)
                if not (first and t == 0):
                    dve.wait_ge(acc_done, q * G + t)
                a = acc[:, bass.ds(at[t], WD)]
                dve.tensor_tensor(a, a, seg(j, t), ALU.add).then_inc(acc_done, 1)

            for q in range(3):
                onehots(q, q, True)
            products(0, 0, 64)
            reduce_heads(0, 0)
            clip(0, 0)

            def steps(i, first, last):
                for j in range(4):
                    s = i * 4 + j
                    old = not (first and j < 2)
                    new = not (last and j == 3)
                    if not (first and j == 0):
                        weight(s - 1, j + 3, False)
                    if not (last and j >= 1):
                        onehots(s + 3, j + 3, first and j == 0)
                    if j == 0:
                        packed = packed_blocks(ET.DVE, 0, 2) if first else packed_blocks(ET.DVE, i * 4 - 2, 4)
                    if old:
                        at = places(packed[j - 2 if first else j], WD)
                    if new:
                        products(s + 1, j + 1, (i + (j + 1) // 4) * 64 + 64)

                    def add(t):
                        if old:
                            accumulate(s - 2, j + 2, t, at, first and j == 2)

                    add(0)
                    if new:
                        reduce_heads(s + 1, j + 1)
                    add(1)
                    if new:
                        clip(s + 1, j + 1)
                    add(2)
                    add(3)

            steps(0, True, False)
            with dve.Fori(1, ITERS - 1) as i:
                steps(i, False, False)
            steps(ITERS - 1, False, True)
            weight(QUADS - 1, 3, False)
            packed = packed_blocks(ET.DVE, QUADS - 2, 2)
            for n in range(2):
                at = places(packed[n], WD)
                for t in range(G):
                    accumulate(QUADS - 2 + n, n, t, at, False)
            dve.wait_ge(acc_done, QUADS * G)

            STEPS_1, STEPS_2 = 7, 3

            def stats(a, u, o, eps, chain, at, done):
                for b in range(XC):
                    ins = dve.bn_stats(stat(u)[:, b, o - 6:o], a[:, b, :])
                ins.then_inc(chain, 1)
                dve.wait_ge(chain, at + 1)
                dve.sem_inc(settled_v, 1)
                for b in range(XC):
                    ins = dve.bn_aggr(stat(u)[:, b, o:o + 2], stat(u)[:, b, o - 6:o])
                ins.then_inc(chain, 1)
                dve.wait_ge(chain, at + 2)
                dve.tensor_scalar(stat(u)[:, :, o + 1], stat(u)[:, :, o + 1], eps, None, ALU.add).then_inc(done, 1)

            def coefs(u, o, std, coef, chain, at, c):
                dve.wait_ge(std, c + 1)
                dve.reciprocal(stat(u)[:, :, o + 3], stat(u)[:, :, o + 2]).then_inc(chain, 1)
                dve.wait_ge(chain, at + 1)
                dve.scalar_tensor_tensor(stat(u)[:, :, o + 4], stat(u)[:, :, o], -1.0, stat(u)[:, :, o + 3],
                                         ALU.mult, ALU.mult).then_inc(coef, 1)

            def head(c, u, i, old, extra):
                at = c * STEPS_1
                sums = acc[:, bass.ds(c * (XC * WD), XC * WD)].rearrange("p (b w) -> p b w", b=XC)
                recip = stat(u)[:, :, 12:12 + H]
                r4 = res(u).rearrange("p b (h e) -> p b h e", h=H)
                s4 = sums[:, :, 0:D].rearrange("p b (h e) -> p b h e", h=H)
                if old:
                    dve.wait_ge(stored[u], 16 * i)
                dve.tensor_scalar(recip, sums[:, :, D:WD], 1e-8, None, ALU.add).then_inc(chain_1, 1)
                dve.wait_ge(chain_1, at + 1)
                dve.reciprocal(recip, recip).then_inc(chain_1, 1)
                dve.wait_ge(chain_1, at + 2)
                dve.tensor_tensor(r4, s4, recip.unsqueeze(3).to_broadcast([P, XC, H, HD]), ALU.mult).then_inc(chain_1, 1)
                dve.wait_ge(chain_1, at + 3)
                dve.wait_ge(xf_in[u], 16 * (i + 1) + extra)
                dve.tensor_tensor(res(u), res(u), xs4[:, u, :, :], ALU.add).then_inc(chain_1, 1)
                dve.wait_ge(chain_1, at + 4)
                stats(res(u), u, 6, 1e-6, chain_1, at + 4, var1)

            def second(c, u):
                dve.wait_ge(res2, c + 1)
                stats(res_b(u), u, 16, 1e-5, chain_2, c * STEPS_2, var2)

            def final(i, slots, old):
                for u in range(slots):
                    c, v = 4 * i + u, (u + 2) % 4
                    ragged = isinstance(i, int) and c == FIN - 1
                    head(c, u, i, old, 16 if ragged else 0)
                    if old or u >= 2:
                        second(c - 2, v)
                    coefs(u, 6, std1, coef1, chain_1, c * STEPS_1 + 6, c)
                    if old or u >= 2:
                        coefs(v, 16, std2, coef2, chain_2, (c - 2) * STEPS_2 + 2, c - 2)

            final(0, 4, False)
            with dve.Fori(1, FIN // 4) as i:
                final(i, 4, True)
            final(FIN // 4, 2, True)
            for c in (FIN, FIN + 1):
                v = (c - 2) % 4
                second(c - 2, v)
                coefs(v, 16, std2, coef2, chain_2, (c - 2) * STEPS_2 + 2, c - 2)


_INS = ["x", "src", "dst", "L0_gnn_qTrans", "L0_gnn_kTrans", "L0_gnn_vTrans", "L0_gnn_ln_scale", "L0_gnn_ln_bias"]
POOL_CONSTS = 10


def kernel(**inputs):
    import numpy as _np
    import concourse.bacc as _bacc
    from concourse import mybir as _mybir
    from concourse.bass_utils import run_bass_kernel_spmd as _run

    nc = _bacc.Bacc("TRN2", target_bir_lowering=False, num_devices=1)
    arrays, args = {}, []
    for name in _INS:
        a = _np.ascontiguousarray(inputs[name])
        arrays[f"in_{name}"] = a
        args.append(nc.dram_tensor(f"in_{name}", a.shape, _mybir.dt.from_np(a.dtype), kind="ExternalInput").ap())
    args.append(nc.dram_tensor("out_0", (NODES, D), _mybir.dt.float32, kind="ExternalOutput").ap())
    build(nc, *args)
    r = _run(nc, [arrays], core_ids=[0])
    return r.results[0]["out_0"]
```

```python
import concourse.bass as bass
from concourse import mybir
from contextlib import ExitStack

P = 128
NODES, EDGES, D, H = 12500, 400000, 128, 8
HD = D // H
NB = -(-NODES // P)
TAIL = NODES - (NB - 1) * P
SIDE = 4096
LOG_P, LOG_ALL = 7, 19
EP = EDGES // P
EGROUPS = -(-EP // P)
GROUPS = EGROUPS + 1
CHG, CHUNKS = 4, 7
assert EP * P == EDGES and NB * (P - 1) <= P * P
assert CHG * (CHUNKS - 1) < EGROUPS and GROUPS <= CHG * CHUNKS and GROUPS * P <= SIDE and GROUPS * P * P <= 1 << LOG_ALL
LOC_SHIFT, BLK_SHIFT = 14, 22
KEY_BASE = 1 << 29
SENT_BIT = 1 << LOC_SHIFT
FILLER = KEY_BASE - (1 << BLK_SHIFT) + SENT_BIT
G = 4
FULL = (EDGES + NB * (P - 1)) // P
TILES = -(-FULL // G) * G
QUADS = TILES // G
ITERS = -(-QUADS // 4)
WD = D + H
KV = 2 * D
CH = 512
XC = 7
NCH = NB // XC
assert NCH * XC == NB


def flat(t, part_elems, off, dims, rows=P):
    dims = [d for d in dims if d[1] > 1] or [[1, 1]]
    return bass.AP(t, off, [[part_elems, rows]] + dims)


def bcast(v):
    return bass.AP(v.tensor, v.offset, [[0, P], [1, D]])


def build(nc, x, src, dst, wq, wk, wv, ln_scale, ln_bias, out):
    f32, bf16, i32 = mybir.dt.float32, mybir.dt.bfloat16, mybir.dt.int32
    ALU, ACT, AX = mybir.AluOpType, mybir.ActivationFunctionType, mybir.AxisListType
    ET = mybir.EngineType
    ctx = ExitStack()
    with ctx:
        def sb(name, shape, dt):
            return ctx.enter_context(nc.sbuf_tensor(name, shape, dt))

        def sem(name):
            return ctx.enter_context(nc.semaphore(name))

        kv_dram = nc.dram_tensor("kv_rows", [NB * P, KV], f32, kind="Internal").ap()

        q_nodes = sb("q_nodes", [P, NB * D], f32)
        acc = sb("acc", [P, NB * WD], f32)
        keys = sb("keys", [P, 2 * SIDE], f32)
        blk_pack = sb("blk_pack", [1, QUADS], i32)
        kv = sb("kv", [P, 4, G, KV], f32)
        prod = sb("prod", [P, G * D], f32)
        wgt = sb("wgt", [P, 2, G, WD], f32)
        onehot = sb("onehot", [P, 4, G * P], bf16)
        onehot32 = sb("onehot32", [P, 2, G * P], f32)
        onehotT = sb("onehotT", [P, 2, G * P], f32)
        att = sb("att", [P, 2, G * H], f32)
        ring = sb("ring", [P, 4, 2, G], i32)
        ident = sb("ident", [P, P], f32)
        ident16 = sb("ident16", [P, P], bf16)
        iota16 = sb("iota16", [P, P], bf16)
        ones = sb("ones", [P, P], f32)
        w_all = sb("w_all", [P, 3 * D], f32)
        xT = sb("xT", [P, 2, P], f32)
        x_tail = sb("x_tail", [P, D], f32)
        part_no = sb("part_no", [P, 1], i32)
        key_const = sb("key_const", [P, 2], i32)
        sign_i = sb("sign_i", [P, LOG_P], i32)
        sign = sb("sign", [P, LOG_P], f32)
        src_in = acc[:, 0:EP].bitcast(i32)
        dst_in = acc[:, SIDE:SIDE + EGROUPS * P].bitcast(i32)
        junk = acc[:, 2 * SIDE:2 * SIDE + (EP + 1) // 2].bitcast(bf16)
        assert 2 * SIDE + (EP + 1) // 2 <= NB * WD
        xs = kv[:, :, :, :].rearrange("p a b c -> p (a b c)")[:, 0:2 * XC * D].rearrange("p (s b d) -> p s b d", s=2, b=XC)
        kv_out_buf = wgt[:, :, :, :].rearrange("p a b c -> p (a b c)")[:, 0:2 * KV].rearrange("p (s c) -> p s c", s=2)
        cnt = onehot32[:, 1, 0:NB + 1]
        thr = onehot32[:, 1, P:P + NB + 1]
        cnt_i = prod[:, P:2 * P].bitcast(i32)
        kv_flat = kv[:, :, :, :].rearrange("p a b c -> p (a b c)")
        blk_parts = [blk_pack[:, :]] + [v[0:1, 0:QUADS] for v in (
            keys[:, SIDE - QUADS:SIDE].bitcast(i32),
            onehot32[:, :, :].rearrange("p a b -> p (a b)").bitcast(i32),
            wgt[:, :, :, :].rearrange("p a b c -> p (a b c)").bitcast(i32))]
        assert QUADS <= 2 * G * P and TILES + QUADS <= SIDE
        small = kv_flat[:, 2 * XC * D:4 * G * KV]
        tri, cols_f, below, at_u, low_v, diff = (small[:, n * P:(n + 1) * P] for n in range(6))
        few_f, few_i = small[:, 6 * P:6 * P + 8], small[:, 6 * P + 8:6 * P + 16].bitcast(i32)
        psum = ctx.enter_context(nc.psum_tensor("psum", [P, 8 * CH], f32))

        def bank(n):
            return psum[:, n * CH:(n + 1) * CH]

        consts = sem("consts")
        const_v = sem("const_v")
        src_in_s, dst_in_s = sem("src_loaded"), sem("dst_loaded")
        w_in, tail_in = sem("w_loaded"), sem("x_tail_loaded")
        x_in = [sem("x_loaded_0"), sem("x_loaded_1")]
        settled_p, settled_v = sem("settled_pool"), sem("settled_dve")
        chain_v = sem("dve_step")
        chain_p = sem("pool_step")
        counted = sem("counted")
        sent_v, sent_pe = sem("sentinels_by_dve"), sem("sentinels_by_pe")
        xt_psum, xt_sb, proj, qkv_sb, q_stored = (sem(n) for n in ("xt_psum", "xt_sb", "projected", "kv_in_sbuf", "q_in_sbuf"))
        kv_out = [sem("kv_stored_0"), sem("kv_stored_1")]
        c_sorted, c_flipped, c_moved = sem("chunk_sorted"), sem("chunk_flipped"), sem("chunk_moved")
        decoded = sem("decoded")
        acc_zero = sem("acc_zero")
        ring_ready, oh_ready, t_ready, ohT_ready, oh32_ready = (sem(n) for n in ("ring_ready", "onehot_ready", "transposed", "onehotT_ready", "onehot32_ready"))
        q_ready, seg_ready, exp_ready = sem("q_gathered"), sem("seg_summed"), sem("exp_ready")
        att_done, w_done, acc_done = sem("att_clipped"), sem("weighted"), sem("accumulated")
        gathered = [sem(f"kv_gathered_{n}") for n in range(4)]
        xf_in = [sem(f"x_again_{n}") for n in range(4)]
        sc_in = sem("scale_loaded")
        stored = [sem(f"out_stored_{n}") for n in range(4)]
        chain_1, chain_2 = sem("first_norm_step"), sem("second_norm_step")
        var1, std1, coef1, norm1, res2, var2, std2, coef2, norm2 = (sem(n) for n in (
            "var1", "std1", "coef1", "norm1", "res2", "var2", "std2", "coef2", "norm2"))
        block = ctx.enter_context(nc.Block())

        def side(buf):
            return buf * SIDE

        PROJECT_AT = range(16, 23)
        FIRST_COUNTS = 28
        COUNTS_AFTER = {1: 6, 3: 6, 4: 2, 5: 6, 6: 3, 7: 6, 8: 4, 9: 6, 10: 5, 11: 6, 12: 6, 13: 6, 14: 7}
        SENT_FLIP = 15
        SENT_PHASE = 17
        assert 1 << (SENT_PHASE - 1 - 2 * LOG_P) <= EGROUPS and (EGROUPS - 1) % (1 << (SENT_PHASE - 1 - 2 * LOG_P)) == 0

        def plan():
            steps = [("T", k, j) for k in range(1, LOG_P + 1) for j in range(k - 1, -1, -1)]
            for k in range(LOG_P + 1, LOG_ALL + 1):
                n = 2 * (k - LOG_P - 1)
                steps.append(("flip", n, k))
                steps += [("R", k, j) for j in range(k - 1, LOG_P - 1, -1)]
                if k < LOG_ALL:
                    steps.append(("flip", n + 1, k))
                    steps += [("T", k, j) for j in range(LOG_P - 1, -1, -1)]
            return steps

        PLAN = plan()

        def groups_in(k):
            return GROUPS if k >= SENT_PHASE else EGROUPS

        def flip_chunks(n):
            k = LOG_P + 1 + n // 2
            total = groups_in(k if n % 2 else k - 1)
            order = {LOG_ALL: [0, 4, 1, 5, 2, 6, 3], LOG_ALL - 1: [0, 2, 1, 3, 4, 6, 5]}.get(k, range(CHUNKS)) if n % 2 == 0 else range(CHUNKS)
            return [(c * CHG, min(CHG, total - c * CHG)) for c in order]

        def buffers():
            at, found = 0, []
            for kind, _, _ in PLAN:
                found.append(at)
                at = 1 - at
            return found + [at]

        BUF = buffers()
        FLIPS = [(s, PLAN[s][1], PLAN[s][2]) for s in range(len(PLAN)) if PLAN[s][0] == "flip"]
        NTR = len(FLIPS)
        END = BUF[-1]
        IDX = 1 - END
        tiles_i = keys[:, side(END):side(END) + TILES].bitcast(i32)
        idx_i = keys[:, side(IDX):side(IDX) + TILES].bitcast(i32)

        def quad_columns(q):
            both = keys[:, :].bitcast(i32).rearrange("p (two c) -> p two c", two=2)
            return both[:, :, bass.ds(q * G, G)]

        FIRST_IS_IDX = IDX == 0
        R_IDX, R_LOC = (0, 1) if FIRST_IS_IDX else (1, 0)

        def seg(j, t):
            return bank(4 + 2 * (j % 2) + t // 2)[:, (t % 2) * WD:(t % 2 + 1) * WD]

        CLAMPED = "each packed block is the minimum of itself and NB - 1, taken on the chip"

        def has(q):
            return not isinstance(q, int) or q < QUADS

        def packed_blocks(engine, first_quad, n):
            return nc.values_load_multi_w_load_instructions(blk_pack[0:1, bass.ds(first_quad, n)], engines=(engine,),
                                                            min_val=0, max_val=(1 << G * LOG_P) - 1,
                                                            skip_runtime_bounds_check_because=CLAMPED)[1]

        def places(packed, width):
            fields = [(packed >> (LOG_P * t)) & (P - 1) if t < G - 1 else packed >> (LOG_P * t) for t in range(G)]
            return [nc.snap(nc.s_assert_within(f, 0, NB - 1, skip_runtime_bounds_check_because=CLAMPED) * width)
                    for f in fields]

        STEPS_1, STEPS_2 = 7, 3
        FIN = NCH
        SLOT = SIDE // 2

        def res(u):
            return keys[:, u * SLOT:u * SLOT + XC * D].rearrange("p (b d) -> p b d", b=XC)

        def res_b(u):
            return keys[:, u * SLOT + XC * D:u * SLOT + 2 * XC * D].rearrange("p (b d) -> p b d", b=XC)

        STAT = 21
        assert 2 * XC * D + XC * STAT <= SLOT

        def stat(u):
            return keys[:, u * SLOT + 2 * XC * D:u * SLOT + 2 * XC * D + XC * STAT].rearrange("p (b s) -> p b s", b=XC)

        xs4 = kv_flat[:, 0:4 * XC * D].rearrange("p (s b d) -> p s b d", s=4, b=XC)

        scale_bc = prod[:, 0:D]
        bias_bc = prod[:, D:2 * D]

        @block.sync
        def _(sp):
            for t, into, done in ((src, src_in, src_in_s), (dst, dst_in[:, 0:EP], dst_in_s)):
                sp.dma_start(into, t.rearrange("(p c) -> p c", p=P)).then_inc(done, 16)
            for n, w in enumerate((wq, wk, wv)):
                sp.dma_start(w_all[:, n * D:(n + 1) * D], w).then_inc(w_in, 16)
            sp.wait_ge(consts, 1)
            sp.dma_start(x_tail[0:TAIL, :], x[(NB - 1) * P:NODES, :]).then_inc(tail_in, 16)

            def load_x(c, nblocks, into, slot, done):
                rows = x[bass.ds(c * XC * P, nblocks * P), :]
                sp.dma_start(into[:, slot, 0:nblocks, :], rows.rearrange("(b p) d -> p b d", p=P)).then_inc(done, 16)

            load_x(0, XC, xs, 0, x_in[0])
            load_x(1, XC, xs, 1, x_in[1])

            def prep(i, last, before_last):
                for u in range(2 * XC):
                    b = i * (2 * XC) + u
                    sp.wait_ge(qkv_sb, b + 1)
                    sp.dma_start(kv_dram[bass.ds(b * P, P), :], kv_out_buf[:, u % 2, :]).then_inc(kv_out[u % 2], 16)
                    if u % XC == XC - 1 and not last:
                        c = 2 * i + (2 if u < XC else 3)
                        sp.wait_ge(xt_psum, b + 1)
                        n = XC - 1 if before_last and u >= XC else XC
                        load_x(c, n, xs, u // XC, x_in[u // XC])

            with sp.Fori(0, NCH // 2 - 2) as i:
                prep(i, False, False)
            prep(NCH // 2 - 2, False, True)
            prep(NCH // 2 - 1, True, False)

            sp.wait_ge(w_done, QUADS)
            sp.dma_start(scale_bc, bcast(ln_scale)).then_inc(sc_in, 16)
            sp.dma_start(bias_bc, bcast(ln_bias)).then_inc(sc_in, 16)

            def load_again(c, u, full, old):
                if old:
                    sp.wait_ge(res2, c - 3)
                rows = XC if full else XC - 1
                load_x(c, rows, xs4, u, xf_in[u])
                if not full:
                    sp.dma_start(xs4[0:TAIL, u, XC - 1, :], x[(NB - 1) * P:NODES, :]).then_inc(xf_in[u], 16)

            def store(c, u, full):
                sp.wait_ge(norm2, c + 1)
                rows = XC if full else XC - 1
                to = out[bass.ds(c * XC * P, rows * P), :]
                sp.dma_start(to.rearrange("(b p) d -> p b d", p=P), res(u)[:, 0:rows, :]).then_inc(stored[u], 16)
                if not full:
                    sp.dma_start(out[(NB - 1) * P:NODES, :], res(u)[0:TAIL, XC - 1, :]).then_inc(stored[u], 16)

            for c in range(4):
                load_again(c, c, True, False)
            with sp.Fori(0, FIN // 4 - 1) as i:
                for u in range(4):
                    store(i * 4 + u, u, True)
                    load_again(i * 4 + 4 + u, u, True, True)
            for c in range(4 * (FIN // 4 - 1), FIN):
                store(c, c % 4, c < FIN - 1)
                if c + 4 < FIN:
                    load_again(c + 4, c % 4, c + 4 < FIN - 1, True)
            for u in range(4):
                sp.wait_ge(stored[u], 16 * len(range(u, FIN, 4)) + (16 if (FIN - 1) % 4 == u else 0))

        @block.gpsimd
        def _(pool):
            steps = [0]

            def link(ins):
                steps[0] += 1
                ins.then_inc(chain_p, 1)
                pool.wait_ge(chain_p, steps[0])

            pool.memset(x_tail[:, :], 0.0).then_inc(consts, 1)
            pool.wait_ge(consts, 1)
            link(pool.iota(part_no[:, :], [[0, 1]], base=0, channel_multiplier=1))
            link(pool.memset(ident[:, :], 0.0))
            link(pool.memset(ones[:, :], 1.0))
            link(pool.affine_select(out=ident[:, :], in_=ident[:, :], compare_op=ALU.not_equal, fill=1.0, base=0,
                                    pattern=[[-1, P]], channel_multiplier=1))
            link(pool.tensor_copy(ident16[:, :], ident[:, :]))
            link(pool.iota(cnt_i[:, 0:P], [[2, P]], base=0, channel_multiplier=0))
            link(pool.tensor_copy(iota16[:, :], cnt_i[:, 0:P]))
            link(pool.iota(cnt_i[:, 0:NB + 1], [[-P, NB + 1]], base=0, channel_multiplier=0))
            link(pool.tensor_copy(thr, cnt_i[:, 0:NB + 1]))
            link(pool.tensor_scalar(thr, thr, 0.5, None, ALU.add))
            link(pool.memset(cnt[:, 0:1], float(EP)))
            link(pool.memset(cnt[:, NB:NB + 1], float(-EP)))
            link(pool.iota(cnt_i[:, 0:P], [[1, P]], base=0, channel_multiplier=0))
            link(pool.tensor_copy(cols_f, cnt_i[:, 0:P]))
            link(pool.memset(tri, 1.0))
            pool.affine_select(out=tri, in_=tri, compare_op=ALU.is_ge, fill=0.0, base=0,
                               pattern=[[-1, P]], channel_multiplier=1).then_inc(consts, 1)
            pool.wait_ge(consts, 2)

            def settle():
                pool.sem_inc(settled_p, 1)

            pool.wait_ge(sent_v, 1)
            pool.memset(acc[:, :], 0.0).then_inc(acc_zero, 1)
            pool.wait_ge(acc_zero, 1)
            base = steps[0]

            for s in range(2):
                pool.wait_ge(kv_out[s], 16 * (NB // 2))

            def gather(i, first):
                for j in range(4):
                    q = i * 4 + j
                    if not has(q):
                        break
                    pool.wait_ge(ring_ready, q + 1)
                    if not first:
                        pool.wait_ge(w_done, q - 3)
                    settle()
                    for t in range(G):
                        pool.indirect_dma_start(kv[:, j, t, :], None, kv_dram,
                                                bass.IndirectOffsetOnAxis(ap=ring[:, j, R_IDX, t:t + 1], axis=0)
                                                ).then_inc(gathered[j], 16)

            gather(0, True)
            with pool.Fori(1, ITERS - 1) as i:
                gather(i, False)
            gather(ITERS - 1, False)

            pool.wait_ge(sc_in, 32)

            def bc(v, n=XC):
                return v.unsqueeze(1).to_broadcast([P, n, D])

            def final(i, slots):
                for u in range(slots):
                    c = 4 * i + u
                    n = c * 2 + base
                    pool.wait_ge(chain_1, c * STEPS_1 + 4)
                    pool.tensor_tensor(xs4[:, u, :, :], xs4[:, u, :, :], bc(bias_bc), ALU.add).then_inc(chain_p, 1)
                    pool.wait_ge(norm1, c + 1)
                    pool.tensor_tensor(res_b(u), res_b(u), bc(scale_bc), ALU.mult).then_inc(chain_p, 1)
                    pool.wait_ge(chain_p, n + 2)
                    pool.tensor_tensor(res_b(u), res_b(u), xs4[:, u, :, :], ALU.add).then_inc(res2, 1)

            with pool.Fori(0, FIN // 4) as i:
                final(i, 4)
            final(FIN // 4, FIN % 4)

        @block.scalar
        def _(act):
            act.wait_ge(chain_p, POOL_CONSTS)
            act.wait_ge(src_in_s, 16)

            def count(t):
                act.activation(junk[:, 0:EP], src_in, ACT.Sign, bias=thr[:, bass.ds(t, 1)], scale=1.0,
                               accum_out=cnt[:, bass.ds(t, 1)]).then_inc(counted, 1)
                act.wait_ge(counted, t)

            with act.Fori(0, 2) as i:
                for u in range(FIRST_COUNTS // 2):
                    count(i * (FIRST_COUNTS // 2) + (u + 1))

            def pair(g, u, first):
                b0 = g * (2 * XC) + 2 * u
                for h in range(2):
                    act.wait_ge(xt_psum, b0 + h + 1)
                    if not first:
                        act.wait_ge(proj, b0 + h - 1)
                    act.activation(xT[:, h, :], bank(h)[:, 0:P], ACT.Copy).then_inc(xt_sb, 1)
                for h in range(2):
                    act.wait_ge(proj, b0 + h + 1)
                    act.activation(q_nodes[:, bass.ds(b0 * D + h * D, D)], bank(2 + h)[:, 0:D], ACT.Copy).then_inc(q_stored, 1)
                    if not first:
                        act.wait_ge(kv_out[h], (u + g * XC) * 16)
                    act.activation(kv_out_buf[:, h, :], bank(2 + h)[:, D:3 * D], ACT.Copy).then_inc(qkv_sb, 1)

            def project(g):
                if g == 0:
                    pair(0, 0, True)
                with act.Fori(1 if g == 0 else 0, XC) as u:
                    pair(g, u, False)

            t = FIRST_COUNTS + 1
            for s, n, k in FLIPS:
                to = side(BUF[s + 1])
                signed = n % 2 == 1 and k < 2 * LOG_P
                sc = sign[:, k - LOG_P:k - LOG_P + 1] if signed else 1.0
                for pos, (g0, ng) in enumerate(flip_chunks(n)):
                    act.wait_ge(c_flipped, CHUNKS * n + pos + 1)
                    act.activation(keys[:, to + g0 * P:to + (g0 + ng) * P], bank(pos)[:, 0:ng * P], ACT.Copy, scale=sc).then_inc(c_moved, 1)
                for u in range(min(COUNTS_AFTER.get(n, 0), NB - t)):
                    count(t)
                    t += 1
                if n in PROJECT_AT:
                    project(n - PROJECT_AT[0])
            assert t == NB

            act.wait_ge(decoded, 1)

            def copy_ring(q, j, gathers):
                if gathers is not None:
                    act.wait_ge(gathered[j], gathers)
                    act.wait_ge(oh_ready, q - 3)
                act.activation(ring[:, j, :, :], quad_columns(q), ACT.Copy).then_inc(ring_ready, 1)

            def expand(q, j, first2):
                act.wait_ge(oh_ready, q + 1)
                if not first2:
                    act.wait_ge(seg_ready, q - 1)
                act.activation(onehot32[:, j % 2, :], onehot[:, j % 4, :], ACT.Copy).then_inc(oh32_ready, 1)

            def exps(q, j, first2):
                act.wait_ge(att_done, q + 1)
                if not first2:
                    act.wait_ge(seg_ready, q - 1)
                a = att[:, j % 2, :].rearrange("p (g h) -> p g h", g=G)
                act.activation(wgt[:, j % 2, :, D:WD], a, ACT.Exp).then_inc(exp_ready, 1)

            def move_T(q, j, first2):
                act.wait_ge(t_ready, q + 1)
                if not first2:
                    act.wait_ge(q_ready, q - 1)
                act.activation(onehotT[:, j % 2, :], bank(j % 2)[:, 0:CH // 2].bitcast(bf16), ACT.Copy).then_inc(ohT_ready, 1)

            for q in range(4):
                copy_ring(q, q, None)
            act.wait_ge(decoded, 2)
            for q in range(3):
                move_T(q, q, q < 2)
            exps(0, 0, True)

            def steps(i, first):
                for j in range(4):
                    s = i * 4 + j
                    if has(s + 4):
                        copy_ring(s + 4, j, i * (16 * G) + 16 * G)
                    if has(s):
                        expand(s, j, first and j < 2)
                    if has(s + 1):
                        exps(s + 1, j + 1, first and j == 0)
                    if has(s + 3):
                        move_T(s + 3, j + 3, False)

            steps(0, True)
            with act.Fori(1, ITERS - 2) as i:
                steps(i, False)
            steps(ITERS - 2, False)
            steps(ITERS - 1, False)

            def root(u, o, var, std, c):
                act.wait_ge(var, c + 1)
                act.activation(stat(u)[:, :, o + 2], stat(u)[:, :, o + 1], ACT.Sqrt).then_inc(std, 1)

            def normalise(u, o, coef, norm, c, a, b):
                act.wait_ge(coef, c + 1)
                for k in range(XC):
                    ins = act.activation(b[:, k, :], a[:, k, :], ACT.Identity, scale=stat(u)[:, k, o + 3:o + 4],
                                         bias=stat(u)[:, k, o + 4:o + 5])
                ins.then_inc(norm, 1)

            def final(i, slots, old, new):
                for u in range(slots):
                    c, v = 4 * i + u, (u + 2) % 4
                    if old or u >= 2:
                        root(v, 16, var2, std2, c - 2)
                    if new:
                        root(u, 6, var1, std1, c)
                    if new:
                        normalise(u, 6, coef1, norm1, c, res(u), res_b(u))
                    if old or u >= 2:
                        normalise(v, 16, coef2, norm2, c - 2, res_b(v), res(v))

            final(0, 4, False, True)
            with act.Fori(1, FIN // 4) as i:
                final(i, 4, True, True)
            final(FIN // 4, 2, True, True)
            for c in (FIN, FIN + 1):
                v = (c - 2) % 4
                root(v, 16, var2, std2, c - 2)
                normalise(v, 16, coef2, norm2, c - 2, res_b(v), res(v))

        @block.tensor
        def _(pe):
            pe.wait_ge(consts, 2)

            def pair(g, u, first, last):
                b0 = g * (2 * XC) + 2 * u
                x14 = kv_flat[:, 0:2 * XC * D]
                for h in range(2):
                    if not first:
                        pe.wait_ge(xt_sb, b0 + h - 1)
                    x_b = x_tail[:, :] if last and h == 1 else x14[:, (2 * u + h) * D:(2 * u + h + 1) * D]
                    pe.transpose(bank(h)[:, 0:P], x_b, ident[:, :]).then_inc(xt_psum, 1)
                for h in range(2):
                    pe.wait_ge(xt_sb, b0 + h + 1)
                    if not first:
                        pe.wait_ge(qkv_sb, b0 + h - 1)
                    pe.matmul(bank(2 + h)[:, 0:3 * D], xT[:, h, :], w_all[:, :], start=True, stop=True).then_inc(proj, 1)

            def project(g):
                pe.wait_ge(x_in[0], 16 * g + 16)
                pe.wait_ge(x_in[1], 16 * g + 16)
                for u in range(XC):
                    pair(g, u, g + u == 0, g == NCH // 2 - 1 and u == XC - 1)
                pe.wait_ge(qkv_sb, (g + 1) * 2 * XC)

            def sentinels():
                own = bank(CHUNKS)
                pe.wait_ge(sent_v, 1)
                pe.matmul(own[0:NB, 0:1], diff[:, 0:NB], ones[:, 0:1], start=True, stop=True).then_inc(sent_pe, 1)
                pe.wait_ge(sent_v, 2)
                pe.matmul(own[0:NB, 0:1], tri[0:NB, 0:NB], few_f[0:NB, 0:1], start=True, stop=True).then_inc(sent_pe, 1)
                pe.wait_ge(sent_v, 3)
                pe.matmul(own[:, P:2 * P], ones[0:NB, :], below[0:NB, :], start=True, stop=False)
                pe.matmul(own[:, P:2 * P], low_v[0:NB, :], at_u[0:NB, :], start=False, stop=True).then_inc(sent_pe, 1)

            for s, n, k in FLIPS:
                at = side(BUF[s])
                for pos, (g0, ng) in enumerate(flip_chunks(n)):
                    pe.wait_ge(c_sorted, CHUNKS * n + pos + 1)
                    if n:
                        pe.wait_ge(c_moved, CHUNKS * (n - 1) + pos + 1)
                    for g in range(ng):
                        o = at + (g0 + g) * P
                        ins = pe.transpose(bank(pos)[:, g * P:(g + 1) * P], keys[:, o:o + P], ident[:, :])
                    ins.then_inc(c_flipped, 1)
                if n == SENT_FLIP:
                    sentinels()
                if n in PROJECT_AT:
                    if n == PROJECT_AT[0]:
                        pe.wait_ge(w_in, 48)
                        pe.wait_ge(tail_in, 16)
                    pe.wait_ge(c_moved, CHUNKS * (n + 1))
                    project(n - PROJECT_AT[0])
            pe.wait_ge(q_stored, NB)

            def transposes(q, j, first2):
                pe.wait_ge(oh_ready, q + 1)
                if not first2:
                    pe.wait_ge(ohT_ready, q - 1)
                for t in range(G):
                    ins = pe.transpose(bank(j % 2)[:, t * P // 2:(t + 1) * P // 2].bitcast(bf16),
                                       onehot[:, j % 4, t * P:(t + 1) * P], ident16[:, :])
                ins.then_inc(t_ready, 1)

            def gather_q(q, j, packed, first2):
                at = places(packed, D)
                pe.wait_ge(ohT_ready, q + 1)
                if not first2:
                    pe.wait_ge(att_done, q - 1)
                for t in range(G):
                    ins = pe.matmul(bank(2 + j % 2)[:, t * D:(t + 1) * D], onehotT[:, j % 2, t * P:(t + 1) * P],
                                    q_nodes[:, bass.ds(at[t], D)], start=True, stop=True)
                ins.then_inc(q_ready, 1)

            def segment_sum(q, j, first2):
                pe.wait_ge(w_done, q + 1)
                pe.wait_ge(oh32_ready, q + 1)
                if not first2:
                    pe.wait_ge(acc_done, (q - 1) * G)
                for t in range(G):
                    ins = pe.matmul(seg(j, t), onehot32[:, j % 2, t * P:(t + 1) * P], wgt[:, j % 2, t, :], start=True, stop=True)
                ins.then_inc(seg_ready, 1)

            for q in range(3):
                transposes(q, q, q < 2)
            pe.wait_ge(decoded, 3)
            early = packed_blocks(ET.PE, 0, 2)
            for q in range(2):
                gather_q(q, q, early[q], True)

            def steps(i, first):
                n = sum(has(i * 4 + 2 + j) for j in range(4))
                if n:
                    later = packed_blocks(ET.PE, i * 4 + 2, n)
                for j in range(4):
                    s = i * 4 + j
                    if has(s + 2):
                        gather_q(s + 2, j + 2, later[j], False)
                    if has(s + 3):
                        transposes(s + 3, j + 3, False)
                    if has(s - 1) and not (first and j == 0):
                        segment_sum(s - 1, j + 3, first and j <= 2)

            steps(0, True)
            with pe.Fori(1, ITERS - 2) as i:
                steps(i, False)
            steps(ITERS - 2, False)
            steps(ITERS - 1, False)
            if QUADS % 4 == 0:
                segment_sum(QUADS - 1, 3, False)

        @block.vector
        def _(dve):
            steps_v = [0]

            def link(ins):
                steps_v[0] += 1
                ins.then_inc(chain_v, 1)
                dve.wait_ge(chain_v, steps_v[0])

            dve.memset(dst_in[:, EP:EGROUPS * P], FILLER)
            dve.wait_ge(chain_p, 1)
            for m in range(LOG_P):
                link(dve.tensor_scalar(sign_i[:, m:m + 1], part_no[:, :], m, 1, ALU.logical_shift_right, ALU.bitwise_and))
            dve.tensor_scalar(sign[:, :], sign_i[:, :], -2.0, 1.0, ALU.mult, ALU.add).then_inc(const_v, 1)
            dve.wait_ge(const_v, 1)
            link(dve.tensor_scalar(key_const[:, 0:1], part_no[:, :], 31, KEY_BASE, ALU.logical_shift_left, ALU.bitwise_or))
            link(dve.tensor_scalar(key_const[:, 1:2], part_no[:, :], 31, None, ALU.logical_shift_left))

            first, other = (keys[:, side(b):side(b) + EGROUPS * P].bitcast(i32) for b in (BUF[0], 1 - BUF[0]))
            dve.tensor_scalar(first[:, EP:], dst_in[:, EP:], key_const[:, 1:2], None, ALU.bitwise_or)
            dve.wait_ge(src_in_s, 16)
            link(dve.tensor_scalar(other[:, 0:EP], src_in, LOC_SHIFT + 1, key_const[:, 0:1], ALU.logical_shift_left, ALU.bitwise_or))
            dve.wait_ge(dst_in_s, 16)
            link(dve.tensor_tensor(first[:, 0:EP], other[:, 0:EP], dst_in[:, 0:EP], ALU.bitwise_or))

            def compare(to, at, o, dist, dims, down, negated=False):
                first_op, second_op = (ALU.max, ALU.min) if down else (ALU.min, ALU.max)
                a, b = (flat(keys, 2 * SIDE, at + o + h, dims) for h in (0, dist))
                low, high = (flat(keys, 2 * SIDE, to + o + h, dims) for h in (0, dist))
                if negated:
                    dve.scalar_tensor_tensor(low, b, -1.0, a, ALU.mult, first_op)
                    return dve.scalar_tensor_tensor(high, b, -1.0, a, ALU.mult, second_op)
                dve.tensor_tensor(low, a, b, first_op)
                return dve.tensor_tensor(high, a, b, second_op)

            def runs(k, g0, ng):
                size = 1 << (k - 2 * LOG_P) if k < LOG_ALL else 2 * GROUPS
                found, g = [], g0
                while g < g0 + ng:
                    n = min((g // size + 1) * size, g0 + ng) - g
                    down = k == LOG_ALL or bool(g // size & 1)
                    for f in found:
                        if (f[1], f[4]) == (n, down) and f[0] + 2 * size * f[3] == g:
                            f[3] += 1
                            break
                    else:
                        found.append([g, n, 2 * size, 1, down])
                    g += n
                return found

            def exchange(to, at, k, j, g0, ng, lanes, negated=False):
                o, n, d = g0 * P, ng * P, 1 << j
                if lanes:
                    return compare(to, at, o, d, [[2 * d, n // (2 * d)], [1, d]], False, negated)
                if k < LOG_P:
                    hi, rest = [2 << k, n >> (k + 1)], [[2 * d, 1 << (k - 1 - j)], [1, d]]
                    if negated or (k - 1 - j > 0 and j > 0 and hi[1] > 1):
                        for start, down in ((0, False), (1 << k, True)):
                            ins = compare(to, at, o + start, d, [hi] + rest, down, negated)
                        return ins
                    dims = [hi, [1 << k, 2]] + rest
                    a, b = (flat(keys, 2 * SIDE, at + o + h, dims) for h in (0, d))
                    dve.tensor_tensor(flat(keys, 2 * SIDE, to + o, [hi, [(1 << k) + d, 2]] + rest), a, b, ALU.min)
                    return dve.tensor_tensor(flat(keys, 2 * SIDE, to + o + d, [hi, [(1 << k) - d, 2]] + rest), a, b, ALU.max)
                for start, size, stride, count, down in runs(k + LOG_P, g0, ng):
                    o, outer = start * P, [stride * P, count]
                    if d < P:
                        ins = compare(to, at, o, d, [outer, [2 * d, size * P // (2 * d)], [1, d]], down, negated)
                        continue
                    whole, rest = divmod(size * P, 2 * d)
                    if whole:
                        ins = compare(to, at, o, d, [outer, [2 * d, whole], [1, d]], down)
                    o += whole * 2 * d
                    both = max(0, rest - d)
                    if both:
                        ins = compare(to, at, o, d, [[1, both]], down)
                    if min(rest, d) > both:
                        ins = dve.tensor_copy(keys[:, to + o + both:to + o + min(rest, d)], keys[:, at + o + both:at + o + min(rest, d)])
                return ins

            def sentinels(part):
                own = bank(CHUNKS)
                if part == 0:
                    dve.wait_ge(consts, 2)
                    dve.wait_ge(counted, NB - 1)
                    dve.tensor_tensor(diff[:, 0:NB], cnt[:, 0:NB], cnt[:, 1:NB + 1], ALU.subtract).then_inc(sent_v, 1)
                    return
                dve.wait_ge(sent_pe, part)
                i, f = few_i[0:NB, :], few_f[0:NB, :]
                if part == 1:
                    link(dve.tensor_scalar(i[:, 0:1], own[0:NB, 0:1], 0.5, None, ALU.mult))
                    link(dve.tensor_scalar(i[:, 0:1], i[:, 0:1], P - 1, None, ALU.bitwise_and))
                    link(dve.tensor_scalar(i[:, 0:1], i[:, 0:1], -1.0, float(P), ALU.mult, ALU.add))
                    link(dve.tensor_scalar(i[:, 0:1], i[:, 0:1], P - 1, None, ALU.bitwise_and))
                    dve.tensor_copy(f[:, 0:1], i[:, 0:1]).then_inc(sent_v, 1)
                if part == 2:
                    link(dve.tensor_copy(i[:, 1:2], own[0:NB, 0:1]))
                    dve.tensor_scalar(i[:, 2:3], i[:, 1:2], LOG_P, None, ALU.logical_shift_right)
                    link(dve.tensor_scalar(i[:, 3:4], i[:, 1:2], P - 1, None, ALU.bitwise_and))
                    link(dve.tensor_copy(f[:, 2:4], i[:, 2:4]))
                    dve.tensor_scalar(below[0:NB, :], cols_f[0:NB, :], f[:, 2:3], None, ALU.is_lt)
                    dve.tensor_scalar(at_u[0:NB, :], cols_f[0:NB, :], f[:, 2:3], None, ALU.is_equal)
                    dve.tensor_scalar(low_v[0:NB, :], cols_f[0:NB, :], f[:, 3:4], None, ALU.is_lt).then_inc(sent_v, 1)
                if part == 3:
                    o = side(BUF[PLAN.index(("R", SENT_PHASE, SENT_PHASE - 1))]) + EGROUPS * P
                    link(dve.tensor_scalar(keys[:, o:o + P].bitcast(i32), own[:, P:2 * P], float(1 << BLK_SHIFT), float(FILLER), ALU.mult, ALU.add))

            for s, (kind, k, j) in enumerate(PLAN):
                if kind == "flip":
                    continue
                at, to = side(BUF[s]), side(BUF[s + 1])
                before, after = PLAN[s - 1] if s else ("", 0, 0), PLAN[s + 1] if s + 1 < len(PLAN) else ("", 0, 0)
                arrives, leaves = before[0] == "flip", after[0] == "flip"
                total = groups_in(k)
                if kind == "R":
                    kk, jj, lanes = k - LOG_P, j - LOG_P, False
                    negated = arrives and k <= 2 * LOG_P
                else:
                    kk, jj, lanes = (k if k < LOG_P else k - LOG_P), j, LOG_P <= k < 2 * LOG_P
                    negated = False
                if arrives and (1 << jj) >= CHG * P:
                    chunks, apart = flip_chunks(before[1]), (1 << jj) // P
                    place = {g0: pos for pos, (g0, _) in enumerate(chunks)}
                    for g0, _ in chunks:
                        if g0 // apart % 2:
                            continue
                        n, n2 = (max(0, min(CHG, total - g)) for g in (g0, g0 + apart))
                        dve.wait_ge(c_moved, CHUNKS * before[1] + max(place[g0], place.get(g0 + apart, 0)) + 1)
                        down = k == LOG_ALL or bool(g0 // (2 * apart) & 1)
                        if n2:
                            ins = compare(to, at, g0 * P, apart * P, [[1, n2 * P]], down)
                        if n > n2:
                            ins = dve.tensor_copy(keys[:, to + (g0 + n2) * P:to + (g0 + n) * P], keys[:, at + (g0 + n2) * P:at + (g0 + n) * P])
                    link(ins)
                elif arrives or leaves:
                    for pos, (g0, ng) in enumerate(flip_chunks(before[1] if arrives else after[1])):
                        if arrives:
                            dve.wait_ge(c_moved, CHUNKS * before[1] + pos + 1)
                        ins = exchange(to, at, kk, jj, g0, ng, lanes, negated)
                        if leaves:
                            ins.then_inc(c_sorted, 1)
                    if not leaves:
                        link(ins)
                else:
                    link(exchange(to, at, kk, jj, 0, total, lanes))
                if (kind, k) == ("T", 7 + SENT_FLIP // 2 + 1) and 2 <= j <= 5:
                    sentinels(5 - j)

            by_quad = tiles_i[0:1, :].rearrange("p (q g) -> p g q", g=G)

            def decode(lo, hi, n):
                for t in range(G):
                    dve.tensor_scalar(blk_parts[t][:, lo:hi], by_quad[:, t, lo:hi], BLK_SHIFT, P - 1, ALU.logical_shift_right, ALU.bitwise_and)
                cols = slice(lo * G, hi * G)
                link(dve.tensor_scalar(idx_i[:, cols], tiles_i[:, cols], (1 << LOC_SHIFT) - 1, None, ALU.bitwise_and))
                dve.tensor_scalar(tiles_i[:, cols], tiles_i[:, cols], LOC_SHIFT, 2 * P - 1, ALU.logical_shift_right,
                                  ALU.bitwise_and).then_inc(decoded, 1)
                dve.wait_ge(decoded, n)

            for n in range(2):
                dve.wait_ge(kv_out[n], 16 * (NB // 2))
            decode(0, 4, 1)
            decode(4, QUADS, 2)

            def onehots(q, j, first):
                dve.wait_ge(ring_ready, q + 1)
                if not first:
                    dve.wait_ge(t_ready, q - 3)
                    dve.wait_ge(oh32_ready, q - 3)
                oh = onehot[:, j % 4, :].rearrange("p (g n) -> p g n", g=G)
                dve.tensor_tensor(oh, iota16[:, :].unsqueeze(1).to_broadcast([P, G, P]),
                                  ring[:, j % 4, R_LOC, :].unsqueeze(2).to_broadcast([P, G, P]), ALU.is_equal
                                  ).then_inc(oh_ready, 1)

            def products(q, j, arrived):
                dve.wait_ge(gathered[j % 4], arrived)
                dve.wait_ge(q_ready, q + 1)
                p = prod[:, :].rearrange("p (g d) -> p g d", g=G)
                ps = bank(2 + j % 2).rearrange("p (g d) -> p g d", g=G)
                dve.tensor_tensor(p, kv[:, j % 4, :, 0:D], ps, ALU.mult).then_inc(chain_v, 1)

            def reduce_heads(q, j):
                dve.wait_ge(chain_v, base_v + 2 * q + 1)
                dve.tensor_reduce(att[:, j % 2, :], prod[:, :].rearrange("p (gh e) -> p gh e", e=HD), AX.X, ALU.add
                                  ).then_inc(chain_v, 1)

            def clip(q, j):
                dve.wait_ge(chain_v, base_v + 2 * q + 2)
                dve.tensor_scalar(att[:, j % 2, :], att[:, j % 2, :], -10.0, 10.0, ALU.max, ALU.min).then_inc(att_done, 1)

            def weight(q, j):
                dve.wait_ge(exp_ready, q + 1)
                w = wgt[:, j % 2, :, 0:D].rearrange("p g (h e) -> p g h e", h=H)
                v = kv[:, j % 4, :, D:KV].rearrange("p g (h e) -> p g h e", h=H)
                e = wgt[:, j % 2, :, D:WD].unsqueeze(3).to_broadcast([P, G, H, HD])
                dve.tensor_tensor(w, v, e, ALU.mult).then_inc(w_done, 1)

            def accumulate(q, j, t, at, first):
                if t == 0:
                    dve.wait_ge(seg_ready, q + 1)
                if not (first and t == 0):
                    dve.wait_ge(acc_done, q * G + t)
                a = acc[:, bass.ds(at[t], WD)]
                dve.tensor_tensor(a, a, seg(j, t), ALU.add).then_inc(acc_done, 1)

            for q in range(3):
                onehots(q, q, True)
            for t in range(G):
                part = blk_parts[t]
                link(dve.tensor_scalar(part, part, float(NB - 1), float(1 << LOG_P * t), ALU.min, ALU.mult))
                if t:
                    ins = dve.tensor_tensor(blk_parts[0], blk_parts[0], part, ALU.bitwise_or)
                    if t < G - 1:
                        link(ins)
            ins.then_inc(decoded, 1)
            dve.wait_ge(decoded, 3)
            base_v = steps_v[0]
            dve.wait_ge(acc_zero, 1)
            products(0, 0, 16 * G)
            reduce_heads(0, 0)
            clip(0, 0)

            def steps(i, first):
                for j in range(4):
                    s = i * 4 + j
                    old = has(s - 2) and not (first and j < 2)
                    new = has(s + 1)
                    if has(s - 1) and not (first and j == 0):
                        weight(s - 1, j + 3)
                    if has(s + 3):
                        onehots(s + 3, j + 3, first and j == 0)
                    if j == 0:
                        start = 0 if first else i * 4 - 2
                        packed = packed_blocks(ET.DVE, start, 2 if first else sum(has(start + n) for n in range(4)))
                    if old:
                        at = places(packed[j - 2 if first else j], WD)
                    if new:
                        products(s + 1, j + 1, (i + (j + 1) // 4) * (16 * G) + 16 * G)

                    def add(t):
                        if old:
                            accumulate(s - 2, j + 2, t, at, first and j == 2)

                    add(0)
                    if new:
                        reduce_heads(s + 1, j + 1)
                    add(1)
                    if new:
                        clip(s + 1, j + 1)
                    add(2)
                    add(3)

            steps(0, True)
            with dve.Fori(1, ITERS - 2) as i:
                steps(i, False)
            steps(ITERS - 2, False)
            steps(ITERS - 1, False)
            left = [q for q in (QUADS - 2, QUADS - 1) if q >= 4 * ITERS - 2]
            if QUADS % 4 == 0:
                weight(QUADS - 1, 3)
            if left:
                packed = packed_blocks(ET.DVE, left[0], len(left))
            for n, q in enumerate(left):
                at = places(packed[n], WD)
                for t in range(G):
                    accumulate(q, q % 4, t, at, False)
            dve.wait_ge(acc_done, QUADS * G)


            def bn(u, a, o, chain):
                for b in range(XC):
                    ins = dve.bn_stats(stat(u)[:, b, o - 6:o], a[:, b, :])
                ins.then_inc(chain, 1)

            def aggregate(u, o, chain, n):
                dve.wait_ge(chain, n)
                dve.sem_inc(settled_v, 1)
                for b in range(XC):
                    ins = dve.bn_aggr(stat(u)[:, b, o:o + 2], stat(u)[:, b, o - 6:o])
                ins.then_inc(chain, 1)

            def add_eps(u, o, eps, chain, n, done):
                dve.wait_ge(chain, n)
                dve.tensor_scalar(stat(u)[:, :, o + 1], stat(u)[:, :, o + 1], eps, None, ALU.add).then_inc(done, 1)

            def inverse(u, o, std, chain, c):
                dve.wait_ge(std, c + 1)
                dve.reciprocal(stat(u)[:, :, o + 3], stat(u)[:, :, o + 2]).then_inc(chain, 1)

            def shift(u, o, coef, chain, n):
                dve.wait_ge(chain, n)
                dve.scalar_tensor_tensor(stat(u)[:, :, o + 4], stat(u)[:, :, o], -1.0, stat(u)[:, :, o + 3],
                                         ALU.mult, ALU.mult).then_inc(coef, 1)

            def step(c, u, i, old, new, extra):
                v = (u + 2) % 4
                n1, n2 = c * STEPS_1, (c - 2) * STEPS_2
                if new:
                    sums = acc[:, bass.ds(c * (XC * WD), XC * WD)].rearrange("p (b w) -> p b w", b=XC)
                    recip = stat(u)[:, :, 12:12 + H]
                    dve.tensor_scalar(recip, sums[:, :, D:WD], 1e-8, None, ALU.add).then_inc(chain_1, 1)
                if old:
                    dve.wait_ge(res2, c - 1)
                    bn(v, res_b(v), 16, chain_2)
                if new:
                    dve.wait_ge(chain_1, n1 + 1)
                    dve.reciprocal(recip, recip).then_inc(chain_1, 1)
                if old:
                    aggregate(v, 16, chain_2, n2 + 1)
                if new:
                    if i is not None:
                        dve.wait_ge(stored[u], 16 * i)
                    dve.wait_ge(chain_1, n1 + 2)
                    dve.tensor_tensor(res(u).rearrange("p b (h e) -> p b h e", h=H),
                                      sums[:, :, 0:D].rearrange("p b (h e) -> p b h e", h=H),
                                      recip.unsqueeze(3).to_broadcast([P, XC, H, HD]), ALU.mult).then_inc(chain_1, 1)
                if old:
                    add_eps(v, 16, 1e-5, chain_2, n2 + 2, var2)
                if new:
                    dve.wait_ge(chain_1, n1 + 3)
                    dve.wait_ge(xf_in[u], 16 * ((0 if i is None else i) + 1) + extra)
                    dve.tensor_tensor(res(u), res(u), xs4[:, u, :, :], ALU.add).then_inc(chain_1, 1)
                    dve.wait_ge(chain_1, n1 + 4)
                    bn(u, res(u), 6, chain_1)
                if old:
                    inverse(v, 16, std2, chain_2, c - 2)
                if new:
                    aggregate(u, 6, chain_1, n1 + 5)
                if old:
                    shift(v, 16, coef2, chain_2, n2 + 3)
                if new:
                    add_eps(u, 6, 1e-6, chain_1, n1 + 6, var1)
                    inverse(u, 6, std1, chain_1, c)
                    shift(u, 6, coef1, chain_1, n1 + 7)

            for c in range(4):
                step(c, c, None, c >= 2, True, 0)
            with dve.Fori(1, FIN // 4) as i:
                for u in range(4):
                    step(4 * i + u, u, i, True, True, 0)
            for c in range(FIN // 4 * 4, FIN):
                step(c, c % 4, FIN // 4, True, True, 16 if c == FIN - 1 else 0)
            for c in (FIN, FIN + 1):
                step(c, c % 4, None, True, False, 0)


_INS = ["x", "src", "dst", "L0_gnn_qTrans", "L0_gnn_kTrans", "L0_gnn_vTrans", "L0_gnn_ln_scale", "L0_gnn_ln_bias"]
POOL_CONSTS = 10


def kernel(**inputs):
    import numpy as _np
    import concourse.bacc as _bacc
    from concourse import mybir as _mybir
    from concourse.bass_utils import run_bass_kernel_spmd as _run

    nc = _bacc.Bacc("TRN2", target_bir_lowering=False, num_devices=1)
    arrays, args = {}, []
    for name in _INS:
        a = _np.ascontiguousarray(inputs[name])
        arrays[f"in_{name}"] = a
        args.append(nc.dram_tensor(f"in_{name}", a.shape, _mybir.dt.from_np(a.dtype), kind="ExternalInput").ap())
    args.append(nc.dram_tensor("out_0", (NODES, D), _mybir.dt.float32, kind="ExternalOutput").ap())
    build(nc, *args)
    r = _run(nc, [arrays], core_ids=[0])
    return r.results[0]["out_0"]
```
